# Optimizing a Trainium2 kernel written in Bass

```python
import numpy as np
import jax
import jax.numpy as jnp

def _softmax(x, axis=-1):
    return jax.nn.softmax(x, axis=axis)

def _gelu(x):
    return jax.nn.gelu(x, approximate=True)

def _silu(x):
    return jax.nn.silu(x)

def _sigmoid(x):
    return jax.nn.sigmoid(x)

def _layernorm(x, axis=-1, eps=1e-05):
    m = jnp.mean(x, axis=axis, keepdims=True)
    v = jnp.var(x, axis=axis, keepdims=True)
    return (x - m) / jnp.sqrt(v + eps)

def _scatter_add(tgt, idx, src, axis=0):
    return tgt.at[idx].add(src)

def _segment_sum(src, seg, n):
    return jax.ops.segment_sum(src, seg, n)
kernel_name = 'mk_recurrent_d1_jaxref_r4_6bab86'

def setup_inputs(seed: int=0):
    np.random.seed(seed)
    _w = jnp.asarray

    def _L0_attn_setup():
        import jax, jax.numpy as jnp
        import numpy as np
        EPS = 1.1920929e-07

        def rmsnorm(x):
            return x * jax.lax.rsqrt(jnp.mean(x * x, axis=-1, keepdims=True) + EPS)

        def mamba_mixer(x, in_proj_w, conv_w, conv_b, x_proj_w, dt_proj_w, dt_proj_b, A_log, D, out_proj_w):
            B_, L, _ = x.shape
            d_inner, d_conv = conv_w.shape
            d_state = A_log.shape[1]
            dt_rank = dt_proj_w.shape[1]
            xz = x @ in_proj_w.T
            xp, z = jnp.split(xz, 2, axis=-1)
            xpad = jnp.pad(xp, ((0, 0), (d_conv - 1, 0), (0, 0)))
            xc = sum((xpad[:, k:k + L, :] * conv_w[:, k] for k in range(d_conv))) + conv_b
            xc = jax.nn.silu(xc)
            x_dbl = xc @ x_proj_w.T
            dt = jax.nn.softplus(x_dbl[..., :dt_rank] @ dt_proj_w.T + dt_proj_b)
            Bm = x_dbl[..., dt_rank:dt_rank + d_state]
            Cm = x_dbl[..., dt_rank + d_state:]
            A = -jnp.exp(A_log)

            def step(h, ts):
                dt_t, B_t, C_t, u_t = ts
                dA = jnp.exp(dt_t[..., None] * A)
                h = h * dA + (dt_t * u_t)[..., None] * B_t[:, None, :]
                y = jnp.einsum('bds,bs->bd', h, C_t)
                return (h, y)
            h0 = jnp.zeros((B_, d_inner, d_state), x.dtype)
            xs = (dt.transpose(1, 0, 2), Bm.transpose(1, 0, 2), Cm.transpose(1, 0, 2), xc.transpose(1, 0, 2))
            _, ys = jax.lax.scan(step, h0, xs)
            y = ys.transpose(1, 0, 2) + xc * D
            y = y * jax.nn.silu(z)
            return y @ out_proj_w.T
        key = jax.random.key(seed)
        ks = jax.random.split(key, 8)
        B, L, d_model = (2, 1024, 256)
        d_state, d_conv, expand = (16, 4, 2)
        d_inner = expand * d_model
        dt_rank = d_model // 16
        s = 0.02
        return {'x': jax.random.normal(ks[0], (B, L, d_model), jnp.float32), 'in_proj_w': jax.random.normal(ks[1], (2 * d_inner, d_model), jnp.float32) * s, 'conv_w': jax.random.normal(ks[2], (d_inner, d_conv), jnp.float32) * 0.2, 'conv_b': jnp.zeros((d_inner,), jnp.float32), 'x_proj_w': jax.random.normal(ks[3], (dt_rank + 2 * d_state, d_inner), jnp.float32) * s, 'dt_proj_w': jax.random.normal(ks[4], (d_inner, dt_rank), jnp.float32) * dt_rank ** (-0.5), 'dt_proj_b': jnp.full((d_inner,), -4.6, jnp.float32), 'A_log': jnp.log(jnp.broadcast_to(jnp.arange(1, d_state + 1, dtype=jnp.float32), (d_inner, d_state))), 'D': jnp.ones((d_inner,), jnp.float32), 'out_proj_w': jax.random.normal(ks[5], (d_model, d_inner), jnp.float32) * s, 'mlp_w1': jax.random.normal(ks[6], (4 * d_model, d_model), jnp.float32) * s, 'mlp_w2': jax.random.normal(ks[7], (d_model, 4 * d_model), jnp.float32) * s}
    _L0_attn_in = _L0_attn_setup()

    def _L0_ffn_setup():
        import jax, jax.numpy as jnp
        import numpy as np
        B, S, D, H, E = (2, 512, 256, 1024, 8)
        TOP_K = 2
        key = jax.random.key(seed)
        ks = jax.random.split(key, 5)
        scale = 0.02
        return {'x': jax.random.normal(ks[0], (B, S, D), dtype=jnp.float32), 'gate_w': jax.random.normal(ks[1], (D, E), dtype=jnp.float32) * scale, 'gate_b': jnp.zeros((E,), dtype=jnp.float32), 'w1': jax.random.normal(ks[2], (E, D, H), dtype=jnp.float32) * scale, 'b1': jnp.zeros((E, H), dtype=jnp.float32), 'w2': jax.random.normal(ks[3], (E, H, D), dtype=jnp.float32) * scale, 'b2': jnp.zeros((E, D), dtype=jnp.float32)}
    _L0_ffn_in = _L0_ffn_setup()
    _d = {'L0_attn_x': _L0_attn_in['x'], 'L0_attn_in_proj_w': _L0_attn_in['in_proj_w'], 'L0_attn_conv_w': _L0_attn_in['conv_w'], 'L0_attn_conv_b': _L0_attn_in['conv_b'], 'L0_attn_x_proj_w': _L0_attn_in['x_proj_w'], 'L0_attn_dt_proj_w': _L0_attn_in['dt_proj_w'], 'L0_attn_dt_proj_b': _L0_attn_in['dt_proj_b'], 'L0_attn_A_log': _L0_attn_in['A_log'], 'L0_attn_D': _L0_attn_in['D'], 'L0_attn_out_proj_w': _L0_attn_in['out_proj_w'], 'L0_attn_mlp_w1': _L0_attn_in['mlp_w1'], 'L0_attn_mlp_w2': _L0_attn_in['mlp_w2'], 'L0_ffn_gate_w': _L0_ffn_in['gate_w'], 'L0_ffn_gate_b': _L0_ffn_in['gate_b'], 'L0_ffn_w1': _L0_ffn_in['w1'], 'L0_ffn_b1': _L0_ffn_in['b1'], 'L0_ffn_w2': _L0_ffn_in['w2'], 'L0_ffn_b2': _L0_ffn_in['b2']}
    _x0 = _d['L0_attn_x']
    _d['L0_attn_x'] = jax.random.normal(jax.random.fold_in(jax.random.key(seed), 1), (2, 2048, 256), dtype=_x0.dtype)
    del _x0
    return _d

def reference(L0_attn_x, L0_attn_in_proj_w, L0_attn_conv_w, L0_attn_conv_b, L0_attn_x_proj_w, L0_attn_dt_proj_w, L0_attn_dt_proj_b, L0_attn_A_log, L0_attn_D, L0_attn_out_proj_w, L0_attn_mlp_w1, L0_attn_mlp_w2, L0_ffn_gate_w, L0_ffn_gate_b, L0_ffn_w1, L0_ffn_b1, L0_ffn_w2, L0_ffn_b2):

    def _L0_attn_ref(x, in_proj_w, conv_w, conv_b, x_proj_w, dt_proj_w, dt_proj_b, A_log, D, out_proj_w, mlp_w1, mlp_w2):
        import jax, jax.numpy as jnp
        import numpy as np
        EPS = 1.1920929e-07

        def rmsnorm(x):
            return x * jax.lax.rsqrt(jnp.mean(x * x, axis=-1, keepdims=True) + EPS)

        def mamba_mixer(x, in_proj_w, conv_w, conv_b, x_proj_w, dt_proj_w, dt_proj_b, A_log, D, out_proj_w):
            B_, L, _ = x.shape
            d_inner, d_conv = conv_w.shape
            d_state = A_log.shape[1]
            dt_rank = dt_proj_w.shape[1]
            xz = x @ in_proj_w.T
            xp, z = jnp.split(xz, 2, axis=-1)
            xpad = jnp.pad(xp, ((0, 0), (d_conv - 1, 0), (0, 0)))
            xc = sum((xpad[:, k:k + L, :] * conv_w[:, k] for k in range(d_conv))) + conv_b
            xc = jax.nn.silu(xc)
            x_dbl = xc @ x_proj_w.T
            dt = jax.nn.softplus(x_dbl[..., :dt_rank] @ dt_proj_w.T + dt_proj_b)
            Bm = x_dbl[..., dt_rank:dt_rank + d_state]
            Cm = x_dbl[..., dt_rank + d_state:]
            A = -jnp.exp(A_log)

            def step(h, ts):
                dt_t, B_t, C_t, u_t = ts
                dA = jnp.exp(dt_t[..., None] * A)
                h = h * dA + (dt_t * u_t)[..., None] * B_t[:, None, :]
                y = jnp.einsum('bds,bs->bd', h, C_t)
                return (h, y)
            h0 = jnp.zeros((B_, d_inner, d_state), x.dtype)
            xs = (dt.transpose(1, 0, 2), Bm.transpose(1, 0, 2), Cm.transpose(1, 0, 2), xc.transpose(1, 0, 2))
            _, ys = jax.lax.scan(step, h0, xs)
            y = ys.transpose(1, 0, 2) + xc * D
            y = y * jax.nn.silu(z)
            return y @ out_proj_w.T
        x = x + mamba_mixer(rmsnorm(x), in_proj_w, conv_w, conv_b, x_proj_w, dt_proj_w, dt_proj_b, A_log, D, out_proj_w)
        x = x + jax.nn.silu(rmsnorm(x) @ mlp_w1.T) @ mlp_w2.T
        return x

    def _L0_ffn_ref(x, gate_w, gate_b, w1, b1, w2, b2):
        import jax, jax.numpy as jnp
        import numpy as np
        B, S, D, H, E = (2, 512, 256, 1024, 8)
        TOP_K = 2
        gate_logits = jnp.einsum('bsd,de->bse', x, gate_w) + gate_b
        gate_weights = jax.nn.softmax(gate_logits, axis=-1)
        topk_values, topk_indices = jax.lax.top_k(gate_weights, TOP_K)
        hidden = jax.nn.relu(jnp.einsum('bsd,edh->bseh', x, w1) + b1)
        expert_out = jnp.einsum('bseh,ehd->bsed', hidden, w2) + b2
        sel = jnp.take_along_axis(expert_out, topk_indices[..., None], axis=2)
        return jnp.sum(topk_values[..., None] * sel, axis=2)
    x = L0_attn_x
    xn = _layernorm(x, axis=-1)
    s = _L0_attn_ref(xn, L0_attn_in_proj_w, L0_attn_conv_w, L0_attn_conv_b, L0_attn_x_proj_w, L0_attn_dt_proj_w, L0_attn_dt_proj_b, L0_attn_A_log, L0_attn_D, L0_attn_out_proj_w, L0_attn_mlp_w1, L0_attn_mlp_w2)
    g = _silu(_L0_ffn_ref(xn, L0_ffn_gate_w, L0_ffn_gate_b, L0_ffn_w1, L0_ffn_b1, L0_ffn_w2, L0_ffn_b2))
    x = x + s * g
    return x

_drawn_inputs = setup_inputs


def setup_inputs(seed=0):
    import zlib

    import numpy as np

    out = dict(_drawn_inputs(seed))
    spreads = {'L0_attn_conv_b': (0.0, 0.1),
     'L0_attn_dt_proj_b': (-4.599999904632568, 0.2),
     'L0_attn_D': (1.0, 0.2),
     'L0_ffn_gate_b': (0.0, 0.1),
     'L0_ffn_b1': (0.0, 0.1),
     'L0_ffn_b2': (0.0, 0.1)}
    factors = {}
    for name, (base, spread) in spreads.items():
        noise = np.random.default_rng([zlib.crc32(name.encode()), seed]).standard_normal(out[name].shape)
        drawn = base * np.exp(spread * noise) if base else spread * noise
        out[name] = jnp.asarray(drawn.astype(out[name].dtype))
    for name, factor in factors.items():
        out[name] = (out[name] * factor).astype(out[name].dtype)
    return out
```

```python
from contextlib import ExitStack

import concourse.bass as bass
from concourse import mybir

F32 = mybir.dt.float32
ALU = mybir.AluOpType
ACT = mybir.ActivationFunctionType
AX_X = mybir.AxisListType.X

P = 128
BATCH, SEQ, DM = 2, 2048, 256
DI = 2 * DM
NS = 16
RK = 16
XD = RK + 2 * NS
TAPS = 4
NE, HID = 8, 1024
BT = 1024
HALVES = SEQ // BT
NT = BT // P
NG = BT // 512
NQ = BT // 256
KC = DM // P
DC = DI // P
HC = HID // P
LN_EPS = 1e-5
RMS_EPS = 1.1920929e-07

P_CONVW = 0
P_CONVB = P_CONVW + DC * TAPS
P_DTB = P_CONVB + DC
P_D = P_DTB + DC
P_ALOG = P_D + DC
P_GATE = P_ALOG + NS * DC
P_XPROJ = P_GATE + KC * NE
P_END = P_XPROJ + DC * XD
W1_COLS = KC * HID + HC
W2_COLS = HC * DM

U_TX = 0
U_TR = U_TX + NG * KC
U_GATE = U_TR + NG * KC
U_IN = U_GATE + 1
U_XD = U_IN + DC * NG
U_CT = U_XD + NG
U_DT = U_CT + 1
U_S = U_DT + DC * NG
PER_S = 10
U_YT = U_S + NS * PER_S
U_Z = U_YT + DC * NG
U_OUT = U_Z + DC * NG
U_T1 = U_OUT + NT
U_MLP = U_T1 + NG * KC
PER_Q = HC // 2 + 1
U_END = U_MLP + NQ * PER_Q
assert U_S % 2 == 0 and U_END % 2 == 0 and PER_S % 2 == 0
BANK_USES = U_END // 2

MOE_ORDER = [(0, 0), (0, 1), (0, 2), (0, 3), (1, 0), (0, None), (1, 1), (1, 2), (1, 3), (1, None)]
K_LAST_UP, K_LAST_DOWN = 8, 9


def mamba_moe(nc, x, params, weights, w_dt, moe1, moe2, moe_b2, gate_b, mlp1, mlp2, out, b_rows):
    with ExitStack() as ctx:
        def sb(name, shape):
            return ctx.enter_context(nc.sbuf_tensor(name, shape, F32))

        def sem(name):
            return ctx.enter_context(nc.semaphore(name))

        par = sb("par", [P, P_END])
        wts = sb("wts", [P, KC * 2 * DI + DC * DM])
        w_in = wts[:, 0:KC * 2 * DI].rearrange("p (k n) -> p k n", k=KC)
        w_out = wts[:, KC * 2 * DI:].rearrange("p (k n) -> p k n", k=DC)
        wdt = sb("wdt", [RK, DI])
        ident = sb("ident", [P, P])
        ones = sb("ones", [1, P])
        gateb = sb("gateb", [P, NE])
        earlier = sb("earlier", [P, NE, NE])
        neg_a = par[:, P_ALOG:P_ALOG + NS * DC]

        xn = sb("xn", [P, NT, DM])
        acc = sb("acc", [P, NT, DI])
        acc_flat = acc[:, :, :].rearrange("p t d -> p (t d)")
        x_sb = acc_flat[:, 0:NT * DM].rearrange("p (t d) -> p t d", t=NT)
        xr = acc_flat[:, NT * DM:2 * NT * DM].rearrange("p (t d) -> p t d", t=NT)
        x1 = xr
        moe = sb("moe", [P, NT, DM])
        xdt = sb("xdt", [P, NT, XD])
        xnT = sb("xnT", [P, KC, BT])
        xrT = sb("xrT", [P, KC, BT])
        xc = sb("xc", [P, DC, BT])
        dt = sb("dt", [P, DC, BT])
        dtu = sb("dtu", [P, DC, BT])
        zs = dt
        yg = dtu
        xdT = sb("xdT", [XD, BT])
        h = sb("h", [P, 2 * DC * BT])
        hst = h[:, :].rearrange("p (b c t) -> p b c t", b=2, c=DC)
        xpad = h[:, 0:DC * (BT + TAPS - 1)].rearrange("p (c t) -> p c t", c=DC)
        x1r = h[:, 0:NT * DM].rearrange("p (t d) -> p t d", t=NT)
        x1rT = h[:, NT * DM:2 * NT * DM].rearrange("p (k t) -> p k t", k=KC)
        res = h[:, 2 * NT * DM:3 * NT * DM].rearrange("p (t d) -> p t d", t=NT)
        halo = sb("halo", [P, DC, TAPS - 1])
        carry = sb("carry", [P, NS * DC])
        bb = sb("bb", [P, 2, BT])
        dbu = sb("dbu", [P, 2, BT])
        w1 = sb("w1", [P, W1_COLS])
        w1v = w1[:, 0:KC * HID].rearrange("p (k n) -> p k n", k=KC)
        w2 = sb("w2", [P, HC, DM])
        b2row = sb("b2row", [1, DM])
        hid = sb("hid", [P, 2, HC, 256])
        st = sb("st", [P, NT, 6])
        mv = sb("mv", [P, NT, 2])
        roots = sb("roots", [P, 2, NT])
        rstd, rr = roots[:, 0, :], roots[:, 1, :]
        ms = sb("ms", [P, NT])
        lg = sb("lg", [P, NT, NE])
        prob = sb("prob", [P, NT, NE])
        red = sb("red", [P, NT])
        cmp = sb("cmp", [P, NT, NE * NE])
        tie = sb("tie", [P, NT, NE * NE])

        decay = ctx.enter_context(nc.psum_tensor("decay", [P, 2, BT], F32))
        hT = ctx.enter_context(nc.psum_tensor("hT", [P, 2, DI], F32))
        mm = ctx.enter_context(nc.psum_tensor("mm", [P, 2, 512], F32))

        params_in = sem("params_in")
        consts = sem("consts")
        aside = sem("aside")
        x_in = sem("x_in")
        x_again = sem("x_again")
        stats = sem("stats")
        xn_ready = sem("xn_ready")
        xr_ready = sem("xr_ready")
        xnT_ready = sem("xnT_ready")
        xrT_ready = sem("xrT_ready")
        nega_ready = sem("nega_ready")
        mm_full = [sem("mm_full0"), sem("mm_full1")]
        mm_free = [sem("mm_free0"), sem("mm_free1")]
        logits_ready = sem("logits_ready")
        exp_ready = sem("exp_ready")
        router = sem("router")
        xp_ready = sem("xp_ready")
        conv = sem("conv")
        xc_ready = sem("xc_ready")
        xdT_ready = sem("xdT_ready")
        xdt_ready = sem("xdt_ready")
        b_out = sem("b_out")
        bb_in = [sem("bb_in0"), sem("bb_in1")]
        softplus = sem("softplus")
        sp_ready = sem("sp_ready")
        dt_ready = sem("dt_ready")
        dtu_ready = sem("dtu_ready")
        acc_zero = sem("acc_zero")
        reset = sem("reset")
        halo_in = sem("halo_in")
        halo_kept = sem("halo_kept")
        decay_ready = sem("decay_ready")
        dbu_ready = sem("dbu_ready")
        scanned = sem("scanned")
        carried = sem("carried")
        hT_ready = sem("hT_ready")
        y_added = sem("y_added")
        w1_in = sem("w1_in")
        w2_in = sem("w2_in")
        hid_ready = sem("hid_ready")
        moe_zero = sem("moe_zero")
        moe_added = sem("moe_added")
        gated = sem("gated")
        y_skip = sem("y_skip")
        z_ready = sem("z_ready")
        yg_ready = sem("yg_ready")
        x1_ready = sem("x1_ready")
        rms = sem("rms")
        rooted = sem("rooted")
        x1r_ready = sem("x1r_ready")
        x1rT_ready = sem("x1rT_ready")
        mlp_hid = sem("mlp_hid")
        s_ready = sem("s_ready")
        prod = sem("prod")
        res_ready = sem("res_ready")
        stored = sem("stored")

        x_t = x.rearrange("(n t p) d -> n p t d", t=NT, p=P)
        out_t = out.rearrange("(n t p) d -> n p t d", t=NT, p=P)

        def full(eng, n, u, s=0):
            eng.wait_ge(mm_full[u % 2], n * BANK_USES + s * (PER_S // 2) + (u // 2 + 1))

        def free(eng, n, u, s=0):
            eng.wait_ge(mm_free[u % 2], n * BANK_USES + s * (PER_S // 2) + (u // 2 + 1))

        def read_out(eng, n, u, s=0):
            eng.wait_ge(mm_free[u % 2], n * BANK_USES + s * (PER_S // 2) + (u // 2 + 2))

        def blocks(eng):
            return eng.Fori(0, BATCH * HALVES)

        def apart(eng):
            eng.sem_inc(aside, 1)

        block = ctx.enter_context(nc.Block())

        @block.sync
        def _(sp):
            sp.dma_start(par[:, :], params).then_inc(params_in, 16)
            sp.dma_start(wts[:, :], weights).then_inc(params_in, 16)
            sp.dma_start(wdt[:, :], w_dt).then_inc(params_in, 16)
            sp.dma_start(gateb[:, :], gate_b.partition_broadcast(P)).then_inc(params_in, 16)

            def load_expert(e):
                sp.dma_start(w1[:, :], moe1[bass.ds(e, 1)].rearrange("a p n -> p (a n)")).then_inc(w1_in, 16)

            def load_expert2(e):
                sp.dma_start(w2[:, :, :].rearrange("p k n -> p (k n)"),
                             moe2[bass.ds(e, 1)].rearrange("a p n -> p (a n)")).then_inc(w2_in, 16)
                sp.dma_start(b2row[:, :], moe_b2[bass.ds(e, 1)]).then_inc(w2_in, 16)

            def load_b(n, s, par_):
                sp.dma_start(bb[:, par_, :],
                             b_rows[bass.ds(n * NS + s, 1), :].rearrange("a t -> (a t)").partition_broadcast(P)
                             ).then_inc(bb_in[par_], 16)

            with blocks(sp) as n:
                sp.wait_ge(res_ready, n * NQ + 1)
                sp.dma_start(x_sb, x_t[bass.ds(n, 1)].rearrange("a p t d -> p (a t) d")).then_inc(x_in, 16)
                full_last = (n * BANK_USES + 1)
                sp.wait_ge(mm_free[0], full_last)
                sp.wait_ge(mm_free[1], full_last)
                load_expert(0)
                load_expert2(0)
                sp.wait_ge(b_out, n * 16 + 16)
                load_b(n, 0, 0)
                load_b(n, 1, 1)

                def after_state(s, par_, e, last_b=False):
                    if not last_b:
                        sp.wait_ge(dbu_ready, n * (NS * DC) + s * DC + DC)
                        load_b(n, s + 2, par_)
                    if par_ == 1:
                        sp.wait_ge(mm_free[0], n * BANK_USES + s * (PER_S // 2) + ((U_S + K_LAST_UP) // 2 + 2))
                        if e is not None:
                            load_expert(e)
                        else:
                            sp.dma_start(w1[:, 0:KC * HID], mlp1).then_inc(w1_in, 16)
                        full(sp, n, U_S + K_LAST_DOWN, s)
                        if e is not None:
                            load_expert2(e)
                        else:
                            sp.dma_start(w2[:, :, :].rearrange("p k n -> p (k n)"), mlp2).then_inc(w2_in, 16)
                            sp.dma_start(b2row[:, :], moe_b2[0:1]).then_inc(w2_in, 16)

                with sp.Fori(0, NS // 2 - 1) as i:
                    after_state(i * 2, 0, None)
                    after_state(i * 2 + 1, 1, i + 1)
                after_state(NS - 1, 1, None, last_b=True)
                sp.wait_ge(z_ready, n * (DC * NG) + DC * NG)
                sp.wait_ge(y_skip, n * (DC * NG) + DC * NG)
                sp.dma_start(x_sb, x_t[bass.ds(n, 1)].rearrange("a p t d -> p (a t) d")).then_inc(x_again, 16)
                sp.wait_ge(res_ready, n * NQ + NQ + 1)
                sp.dma_start(out_t[bass.ds(n, 1)].rearrange("a p t d -> p (a t) d"), res).then_inc(stored, 16)
                sp.wait_ge(stored, n * 16 + 16)
                apart(sp)

        @block.gpsimd
        def _(pool):
            nc.gpsimd.memset(ident[:, :], 0.0).then_inc(consts, 1)
            nc.gpsimd.memset(earlier[:, :, :], 0.0).then_inc(consts, 1)
            nc.gpsimd.memset(ones[:, :], 1.0).then_inc(consts, 1)
            pool.wait_ge(consts, 3)
            nc.gpsimd.affine_select(out=ident[:, :], in_=ident[:, :], compare_op=ALU.not_equal, fill=1.0,
                                    base=0, pattern=[[-1, P]], channel_multiplier=1).then_inc(consts, 1)
            nc.gpsimd.affine_select(out=earlier[:, :, :], in_=earlier[:, :, :], compare_op=ALU.is_ge, fill=1.0,
                                    base=0, pattern=[[-1, NE], [1, NE]], channel_multiplier=0).then_inc(consts, 1)

            with blocks(pool) as n:
                pool.wait_ge(dtu_ready, n * DC + DC)
                apart(pool)
                with pool.Fori(0, NS // 2) as i:
                    for half in range(2):
                        pool.wait_ge(bb_in[half], n * (NS * 8) + i * 16 + 16)
                        for c in range(DC):
                            pool.wait_ge(scanned, n * (NS * DC) + i * (2 * DC) + (half * DC + c + 1))
                            nc.gpsimd.tensor_tensor(dbu[:, c % 2, :], dtu[:, c, :], bb[:, half, :],
                                                    ALU.mult).then_inc(dbu_ready, 1)

        @block.scalar
        def _(act):
            act.wait_ge(params_in, 64)
            nc.scalar.activation(neg_a, neg_a, ACT.Exp).then_inc(nega_ready, 1)
            act.wait_ge(nega_ready, 1)
            nc.scalar.mul(neg_a, neg_a, -1.0).then_inc(nega_ready, 1)
            act.wait_ge(nega_ready, 2)

            with blocks(act) as n:
                act.wait_ge(stats, n * 7 + 7)
                nc.scalar.activation(roots[:, :, :], roots[:, :, :], ACT.Sqrt).then_inc(rooted, 1)
                for g in range(NG):
                    for k in range(KC):
                        u = U_TX + g * KC + k
                        full(act, n, u)
                        nc.scalar.copy(xnT[:, k, g * 512:g * 512 + 512], mm[:, u % 2, :]).then_inc(mm_free[u % 2], 1)
                for g in range(NG):
                    for k in range(KC):
                        u = U_TR + g * KC + k
                        full(act, n, u)
                        nc.scalar.copy(xrT[:, k, g * 512:g * 512 + 512], mm[:, u % 2, :]).then_inc(mm_free[u % 2], 1)
                act.wait_ge(halo_in, n + 1)
                for c in range(DC):
                    for g in range(NG):
                        u = U_IN + c * NG + g
                        full(act, n, u)
                        o = TAPS - 1 + g * 512
                        nc.scalar.copy(xpad[:, c, o:o + 512], mm[:, u % 2, :]).then_inc(mm_free[u % 2], 1)
                act.wait_ge(logits_ready, n + 1)
                nc.scalar.activation(lg[:, :, :], lg[:, :, :], ACT.Exp).then_inc(exp_ready, 1)
                for c in range(DC):
                    act.wait_ge(conv, n * (DC * TAPS) + (c + 1) * TAPS)
                    nc.scalar.activation(xc[:, c, :], xc[:, c, :], ACT.Silu).then_inc(xc_ready, 1)
                for g in range(NG):
                    u = U_XD + g
                    full(act, n, u)
                    nc.scalar.copy(xdT[:, g * 512:g * 512 + 512], mm[0:XD, u % 2, :]).then_inc(mm_free[u % 2], 1)
                for g in range(NG):
                    read_out(act, n, U_XD + g)
                act.dma_start(b_rows[bass.ds(n * NS, NS), :], xdT[RK:RK + NS, :]).then_inc(b_out, 16)
                for c in range(DC):
                    for g in range(NG):
                        u = U_DT + c * NG + g
                        cols = slice(g * 512, g * 512 + 512)
                        full(act, n, u)
                        bias = par[:, P_DTB + c:P_DTB + c + 1]
                        nc.scalar.activation(dt[:, c, cols], mm[:, u % 2, :], ACT.Abs, bias=bias).then_inc(softplus, 1)
                        nc.scalar.activation(dtu[:, c, cols], mm[:, u % 2, :], ACT.Relu,
                                             bias=bias).then_inc(mm_free[u % 2], 1)
                per = DC * NG + DC
                for c in range(DC):
                    act.wait_ge(softplus, n * per + DC * NG)
                    nc.scalar.activation(dt[:, c, :], dt[:, c, :], ACT.Exp, scale=-1.0).then_inc(softplus, 1)
                for c in range(DC):
                    act.wait_ge(softplus, n * per + DC * NG + c + 1)
                    nc.scalar.activation(dt[:, c, :], dt[:, c, :], ACT.Ln, bias=1.0).then_inc(sp_ready, 1)
                act.wait_ge(dt_ready, n * DC + DC)

                def state(s):
                    for c in range(DC):
                        act.wait_ge(scanned, n * (NS * DC) + s * DC + (c + 1))
                        nc.scalar.activation(decay[:, c % 2, :], dt[:, c, :], ACT.Exp,
                                             scale=par[:, bass.ds(s * DC + (P_ALOG + c), 1)]).then_inc(decay_ready, 1)
                        for k in [(0, 1), (2, 3), (4, 6), (7, 8)][c]:
                            unit, pair = MOE_ORDER[k]
                            full(act, n, U_S + k, s)
                            for m in range(2):
                                hc = 2 * pair + m
                                last = nc.scalar.activation(hid[:, unit, hc, :], mm[:, k % 2, m * 256:m * 256 + 256],
                                                            ACT.Relu, bias=w1[:, KC * HID + hc:KC * HID + hc + 1])
                            last.then_inc(mm_free[k % 2], 1)

                with act.Fori(0, NS) as s:
                    state(s)
                act.wait_ge(moe_added, n * (NS * 4) + NS * 4)
                nc.scalar.activation(moe[:, :, :], moe[:, :, :], ACT.Silu).then_inc(gated, 1)
                for c in range(DC):
                    for g in range(NG):
                        u = U_Z + c * NG + g
                        full(act, n, u)
                        nc.scalar.activation(zs[:, c, g * 512:g * 512 + 512], mm[:, u % 2, :], ACT.Silu).then_inc(z_ready, 1)
                        act.wait_ge(z_ready, n * (DC * NG) + c * NG + g + 1)
                        act.sem_inc(mm_free[u % 2], 1)
                act.wait_ge(rms, n * 6 + 6)
                nc.scalar.activation(rr, rr, ACT.Sqrt).then_inc(rooted, 1)
                for g in range(NG):
                    for k in range(KC):
                        u = U_T1 + g * KC + k
                        full(act, n, u)
                        nc.scalar.copy(x1rT[:, k, g * 512:g * 512 + 512], mm[:, u % 2, :]).then_inc(mm_free[u % 2], 1)
                for q in range(NQ):
                    for pair in range(HC // 2):
                        u = U_MLP + q * PER_Q + pair
                        full(act, n, u)
                        nc.scalar.activation(hid[:, q % 2, 2 * pair:2 * pair + 2, :],
                                             mm[:, u % 2, :].rearrange("p (m t) -> p m t", m=2),
                                             ACT.Silu).then_inc(mm_free[u % 2], 1)

        @block.tensor
        def _(pe):
            pe.wait_ge(params_in, 64)
            pe.wait_ge(consts, 5)

            def transposes(n, u, pieces):
                free(pe, n, u)
                for i, src in enumerate(pieces):
                    last = pe.transpose(mm[:, u % 2, i * P:i * P + P], src, ident[:, :])
                last.then_inc(mm_full[u % 2], 1)

            def up(bank, xT, cols, pair):
                for m in range(2):
                    hc = 2 * pair + m
                    for k in range(KC):
                        last = pe.matmul(mm[:, bank, m * 256:m * 256 + 256], w1v[:, k, hc * P:hc * P + P],
                                         xT[:, k, cols], start=(k == 0), stop=(k == KC - 1))
                return last

            def down(bank, unit, with_bias):
                for m in range(2):
                    o = mm[:, bank, m * DM:m * DM + DM]
                    for hc in range(HC):
                        last = pe.matmul(o, hid[:, unit, hc, m * P:m * P + P], w2[:, hc, :],
                                         start=(hc == 0), stop=(hc == HC - 1 and not with_bias))
                    if with_bias:
                        last = pe.matmul(o, ones[:, :], b2row[:, :], start=False, stop=True)
                return last

            with blocks(pe) as n:
                for g in range(NG):
                    pe.wait_ge(xn_ready, n * NT + g * 4 + 4)
                    for k in range(KC):
                        transposes(n, U_TX + g * KC + k, [xn[:, g * 4 + j, k * P:k * P + P] for j in range(4)])
                for g in range(NG):
                    pe.wait_ge(xr_ready, n * NT + g * 4 + 4)
                    for k in range(KC):
                        transposes(n, U_TR + g * KC + k, [xr[:, g * 4 + j, k * P:k * P + P] for j in range(4)])
                for u in (U_TR - 2, U_TR - 1):
                    read_out(pe, n, u)
                free(pe, n, U_GATE)
                for j in range(NT):
                    for k in range(KC):
                        last = pe.matmul(mm[:, U_GATE % 2, j * NE:j * NE + NE], xnT[:, k, j * P:j * P + P],
                                         par[:, P_GATE + k * NE:P_GATE + k * NE + NE],
                                         start=(k == 0), stop=(k == KC - 1))
                last.then_inc(mm_full[U_GATE % 2], 1)
                for u in (U_GATE - 2, U_GATE - 1):
                    read_out(pe, n, u)

                def in_proj(u, c, g):
                    free(pe, n, u)
                    for k in range(KC):
                        last = pe.matmul(mm[:, u % 2, :], w_in[:, k, c * P:c * P + P], xrT[:, k, g * 512:g * 512 + 512],
                                         start=(k == 0), stop=(k == KC - 1))
                    last.then_inc(mm_full[u % 2], 1)

                for c in range(DC):
                    for g in range(NG):
                        in_proj(U_IN + c * NG + g, c, g)
                pe.wait_ge(xc_ready, n * DC + DC)
                for g in range(NG):
                    u = U_XD + g
                    free(pe, n, u)
                    for c in range(DC):
                        last = pe.matmul(mm[0:XD, u % 2, :], par[:, P_XPROJ + c * XD:P_XPROJ + c * XD + XD],
                                         xc[:, c, g * 512:g * 512 + 512], start=(c == 0), stop=(c == DC - 1))
                    last.then_inc(mm_full[u % 2], 1)
                for g in range(NG):
                    read_out(pe, n, U_XD + g)
                free(pe, n, U_CT)
                apart(pe)
                for j in range(NT):
                    last = pe.transpose(mm[:, U_CT % 2, j * XD:j * XD + XD], xdT[:, j * P:j * P + P], ident[0:XD, 0:XD])
                last.then_inc(mm_full[U_CT % 2], 1)
                for c in range(DC):
                    for g in range(NG):
                        u = U_DT + c * NG + g
                        free(pe, n, u)
                        pe.matmul(mm[:, u % 2, :], wdt[:, c * P:c * P + P], xdT[0:RK, g * 512:g * 512 + 512],
                                  start=True, stop=True).then_inc(mm_full[u % 2], 1)

                def state_tile(s, par_, j):
                    if j == 0:
                        pe.wait_ge(scanned, n * (NS * DC) + s * DC + (DC + 2))
                    pe.wait_ge(y_added, n * (NS * NT) + s * NT + (j + 1))
                    for c in range(DC):
                        last = pe.transpose(hT[:, j % 2, c * P:c * P + P], hst[:, par_, c, j * P:j * P + P], ident[:, :])
                    last.then_inc(hT_ready, 1)

                def moe_use(s, par_, e, k):
                    unit, pair = MOE_ORDER[k]
                    q = 2 * par_ + unit
                    free(pe, n, U_S + k, s)
                    if k == 0 and par_ == 0:
                        pe.wait_ge(w1_in, n * ((NE + 1) * 16) + e * 16 + 16)
                    if k == 5 and par_ == 0:
                        pe.wait_ge(w2_in, n * ((NE + 1) * 32) + e * 32 + 32)
                    if pair is not None:
                        last = up(k % 2, xnT, slice(q * 256, q * 256 + 256), pair)
                    else:
                        kk = 3 if unit == 0 else 8
                        read_out(pe, n, U_S + kk, s)
                        read_out(pe, n, U_S + kk - 1, s)
                        last = down(k % 2, unit, True)
                    last.then_inc(mm_full[k % 2], 1)

                def step(s, par_, e, tiles, moes):
                    k = 0
                    for j in range(NT):
                        if moes:
                            for _ in range(2 if j in (0, 4) else 1):
                                moe_use(s, par_, e, k)
                                k += 1
                        if tiles:
                            state_tile(s - 1, 1 - par_, j)

                step(0, 0, 0, False, True)
                with pe.Fori(0, NS // 2 - 1) as i:
                    step(i * 2 + 1, 1, i, True, True)
                    step(i * 2 + 2, 0, i + 1, True, True)
                step(NS - 1, 1, NE - 1, True, True)
                step(NS, 0, None, True, False)

                for c in range(DC):
                    for g in range(NG):
                        if c == 0:
                            pe.wait_ge(y_added, n * (NS * NT) + (NS - 1) * NT + g * 4 + 4 + 2)
                        transposes(n, U_YT + c * NG + g, [acc[:, g * 4 + j, c * P:c * P + P] for j in range(4)])
                for c in range(DC):
                    for g in range(NG):
                        in_proj(U_Z + c * NG + g, DC + c, g)
                pe.wait_ge(yg_ready, n * (DC * NG) + DC * NG)
                for j in range(NT):
                    u = U_OUT + j
                    free(pe, n, u)
                    for c in range(DC):
                        last = pe.matmul(mm[:, u % 2, 0:DM], yg[:, c, j * P:j * P + P], w_out[:, c, :],
                                         start=(c == 0), stop=(c == DC - 1))
                    last.then_inc(mm_full[u % 2], 1)
                for g in range(NG):
                    pe.wait_ge(x1r_ready, n * NT + g * 4 + 4)
                    for k in range(KC):
                        transposes(n, U_T1 + g * KC + k, [x1r[:, g * 4 + j, k * P:k * P + P] for j in range(4)])
                read_out(pe, n, U_MLP - 2)
                read_out(pe, n, U_MLP - 1)
                pe.wait_ge(w1_in, n * ((NE + 1) * 16) + (NE + 1) * 16)
                pe.wait_ge(w2_in, n * ((NE + 1) * 32) + (NE + 1) * 32)
                for q in range(NQ):
                    for pair in range(HC // 2):
                        u = U_MLP + q * PER_Q + pair
                        free(pe, n, u)
                        up(u % 2, x1rT, slice(q * 256, q * 256 + 256), pair).then_inc(mm_full[u % 2], 1)
                    u = U_MLP + q * PER_Q + HC // 2
                    read_out(pe, n, u - 2)
                    read_out(pe, n, u - 1)
                    free(pe, n, u)
                    down(u % 2, q % 2, False).then_inc(mm_full[u % 2], 1)

        @block.vector
        def _(dve):
            for s_, v in ((mm_free[0], 1), (mm_free[1], 1), (scanned, 2), (y_added, 2), (res_ready, 1)):
                dve.sem_inc(s_, v)
            dve.wait_ge(params_in, 64)
            dve.wait_ge(consts, 5)

            STATS = 7

            def a_block(n):
                dve.wait_ge(x_in, n * 16 + 16)
                for j in range(NT):
                    last = nc.vector.bn_stats(st[:, j, :], x_sb[:, j, :])
                last.then_inc(stats, 1)
                dve.wait_ge(stats, n * STATS + 1)
                apart(dve)
                for j in range(NT):
                    last = nc.vector.bn_aggr(mv[:, j, :], st[:, j, :])
                last.then_inc(stats, 1)
                dve.wait_ge(stats, n * STATS + 2)
                nc.vector.tensor_scalar(ms[:, :], mv[:, :, 1], LN_EPS, None, ALU.add).then_inc(stats, 1)
                dve.wait_ge(stats, n * STATS + 3)
                nc.vector.reciprocal(rstd, ms[:, :]).then_inc(stats, 1)
                dve.wait_ge(stats, n * STATS + 4)
                nc.vector.tensor_tensor(ms[:, :], mv[:, :, 1], rstd, ALU.mult).then_inc(stats, 1)
                dve.wait_ge(stats, n * STATS + 5)
                nc.vector.tensor_scalar(ms[:, :], ms[:, :], RMS_EPS, None, ALU.add).then_inc(stats, 1)
                dve.wait_ge(stats, n * STATS + 6)
                nc.vector.reciprocal(rr, ms[:, :]).then_inc(stats, 1)
                dve.wait_ge(rooted, n * 2 + 1)
                for j in range(NT):
                    nc.vector.tensor_scalar(xn[:, j, :], x_sb[:, j, :], mv[:, j, 0:1], roots[:, 0, j:j + 1],
                                            ALU.subtract, ALU.mult).then_inc(xn_ready, 1)
                dve.wait_ge(xn_ready, n * NT + NT)
                for j in range(NT):
                    nc.vector.tensor_scalar(xr[:, j, :], xn[:, j, :], roots[:, 1, j:j + 1], None, ALU.mult).then_inc(xr_ready, 1)

                R = 9
                full(dve, n, U_GATE)
                gb = gateb[:, :].rearrange("p (a e) -> p a e", a=1).broadcast_to([P, NT, NE])
                nc.vector.tensor_tensor(lg[:, :, :], mm[:, U_GATE % 2, 0:NT * NE].rearrange("p (t e) -> p t e", t=NT),
                                        gb, ALU.add).then_inc(mm_free[U_GATE % 2], 1)
                read_out(dve, n, U_GATE)
                nc.vector.tensor_reduce(red[:, :], lg[:, :, :], AX_X, ALU.max).then_inc(router, 1)
                dve.wait_ge(router, n * R + 1)
                redb = red[:, :].rearrange("p (t a) -> p t a", a=1).broadcast_to([P, NT, NE])
                nc.vector.tensor_tensor(lg[:, :, :], lg[:, :, :], redb, ALU.subtract).then_inc(logits_ready, 1)

                dve.wait_ge(halo_in, n + 1)
                for c in range(DC):
                    for g in range(NG):
                        read_out(dve, n, U_IN + c * NG + g)
                    w = [par[:, P_CONVW + c * TAPS + k:P_CONVW + c * TAPS + k + 1] for k in range(TAPS)]
                    nc.vector.tensor_scalar(xc[:, c, :], xpad[:, c, 0:BT], w[0], par[:, P_CONVB + c:P_CONVB + c + 1],
                                            ALU.mult, ALU.add).then_inc(conv, 1)
                    for k in range(1, TAPS):
                        dve.wait_ge(conv, n * (DC * TAPS) + c * TAPS + k)
                        nc.vector.scalar_tensor_tensor(out=xc[:, c, :], in0=xpad[:, c, k:k + BT], scalar=w[k],
                                                       in1=xc[:, c, :], op0=ALU.mult, op1=ALU.add).then_inc(conv, 1)
                nc.vector.tensor_copy(halo[:, :, :], xpad[:, :, BT:BT + TAPS - 1]).then_inc(halo_kept, 1)

                dve.wait_ge(exp_ready, n + 1)
                nc.vector.tensor_reduce(red[:, :], lg[:, :, :], AX_X, ALU.add).then_inc(router, 1)
                dve.wait_ge(router, n * R + 2)
                nc.vector.reciprocal(red[:, :], red[:, :]).then_inc(router, 1)
                dve.wait_ge(router, n * R + 3)
                nc.vector.tensor_tensor(prob[:, :, :], lg[:, :, :], redb, ALU.mult).then_inc(router, 1)
                dve.wait_ge(router, n * R + 4)
                for j in range(NT):
                    this = prob[:, j, :].rearrange("p (e a) -> p e a", a=1).broadcast_to([P, NE, NE])
                    other = prob[:, j, :].rearrange("p (a e) -> p a e", a=1).broadcast_to([P, NE, NE])
                    nc.vector.tensor_tensor(cmp[:, j, :].rearrange("p (e f) -> p e f", e=NE), other, this, ALU.is_gt)
                    last = nc.vector.tensor_tensor(tie[:, j, :].rearrange("p (e f) -> p e f", e=NE), other, this,
                                                   ALU.is_equal)
                last.then_inc(router, 1)
                dve.wait_ge(router, n * R + 5)
                eb = earlier[:, :, :].rearrange("p (a e) f -> p a (e f)", a=1).broadcast_to([P, NT, NE * NE])
                nc.vector.tensor_tensor(tie[:, :, :], tie[:, :, :], eb, ALU.mult).then_inc(router, 1)
                dve.wait_ge(router, n * R + 6)
                nc.vector.tensor_tensor(cmp[:, :, :], cmp[:, :, :], tie[:, :, :], ALU.add).then_inc(router, 1)
                dve.wait_ge(router, n * R + 7)
                nc.vector.tensor_reduce(lg[:, :, :], cmp[:, :, :].rearrange("p t (e f) -> p t e f", e=NE), AX_X,
                                        ALU.add).then_inc(router, 1)
                dve.wait_ge(router, n * R + 8)
                nc.vector.scalar_tensor_tensor(out=prob[:, :, :], in0=lg[:, :, :], scalar=1.5, in1=prob[:, :, :],
                                               op0=ALU.is_lt, op1=ALU.mult).then_inc(router, 1)
                nc.vector.memset(moe[:, :, :], 0.0).then_inc(moe_zero, 1)
                full(dve, n, U_CT)
                nc.vector.tensor_copy(xdt[:, :, :].rearrange("p t d -> p (t d)"),
                                      mm[:, U_CT % 2, 0:NT * XD]).then_inc(mm_free[U_CT % 2], 1)
                read_out(dve, n, U_CT)
                nc.vector.memset(acc[:, :, :], 0.0).then_inc(acc_zero, 1)
                for c in range(DC):
                    dve.wait_ge(sp_ready, n * DC + c + 1)
                    nc.vector.tensor_tensor(dt[:, c, :], dt[:, c, :], dtu[:, c, :], ALU.add).then_inc(dt_ready, 1)
                for c in range(DC):
                    dve.wait_ge(dt_ready, n * DC + c + 1)
                    nc.vector.tensor_tensor(dtu[:, c, :], dt[:, c, :], xc[:, c, :], ALU.mult).then_inc(dtu_ready, 1)
                dve.wait_ge(router, n * R + 9)
                dve.wait_ge(moe_zero, n + 1)
                dve.wait_ge(acc_zero, n + 1)
                dve.wait_ge(halo_kept, n + 1)

            def scan(n, s, par_, c):
                dve.wait_ge(decay_ready, n * (NS * DC) + s * DC + (c + 1))
                dve.wait_ge(dbu_ready, n * (NS * DC) + s * DC + (c + 1))
                nc.vector.tensor_tensor_scan(hst[:, par_, c, :], decay[:, c % 2, :], dbu[:, c % 2, :],
                                             carry[:, bass.ds(s * DC + c, 1)], ALU.mult, ALU.add).then_inc(scanned, 1)

            def keep(n, s, par_):
                dve.wait_ge(scanned, n * (NS * DC) + s * DC + (DC + 2))
                apart(dve)
                nc.vector.tensor_copy(carry[:, bass.ds(s * DC, DC)], hst[:, par_, :, BT - 1]).then_inc(carried, 1)

            def add_y(n, s, j):
                dve.wait_ge(hT_ready, n * (NS * NT) + s * NT + (j + 1))
                nc.vector.scalar_tensor_tensor(out=acc[:, j, :], in0=hT[:, j % 2, :],
                                               scalar=xdt[:, j, bass.ds(s + (RK + NS), 1)], in1=acc[:, j, :],
                                               op0=ALU.mult, op1=ALU.add).then_inc(y_added, 1)

            def add_moe(n, s, par_, e, k):
                unit, _ = MOE_ORDER[k]
                full(dve, n, U_S + k, s)
                if unit == 0:
                    dve.wait_ge(moe_added, n * (NS * 4) + s * 4)
                for m in range(2):
                    j = 2 * (2 * par_ + unit) + m
                    last = nc.vector.scalar_tensor_tensor(out=moe[:, j, :], in0=mm[:, k % 2, m * DM:m * DM + DM],
                                                          scalar=prob[:, j, bass.ds(e, 1)], in1=moe[:, j, :],
                                                          op0=ALU.mult, op1=ALU.add)
                    last.then_inc(moe_added if m == 0 else moe_added, 1)
                dve.wait_ge(moe_added, n * (NS * 4) + s * 4 + (2 * unit + 2))
                dve.sem_inc(mm_free[k % 2], 1)

            def step(n, s, par_, e, scans, adds):
                for c in range(DC):
                    if scans:
                        scan(n, s, par_, c)
                    for j in (2 * c, 2 * c + 1):
                        if adds:
                            add_y(n, s - 1, j)
                        if scans and j == 4:
                            add_moe(n, s, par_, e, 5)
                if scans:
                    keep(n, s, par_)
                    add_moe(n, s, par_, e, 9)

            def c_block(n):
                for c in range(DC):
                    for g in range(NG):
                        u = U_YT + c * NG + g
                        cols = slice(g * 512, g * 512 + 512)
                        full(dve, n, u)
                        nc.vector.scalar_tensor_tensor(out=yg[:, c, cols], in0=xc[:, c, cols],
                                                       scalar=par[:, P_D + c:P_D + c + 1], in1=mm[:, u % 2, :],
                                                       op0=ALU.mult, op1=ALU.add).then_inc(y_skip, 1)
                        dve.wait_ge(y_skip, n * (DC * NG) + c * NG + g + 1)
                        dve.sem_inc(mm_free[u % 2], 1)
                for c in range(DC):
                    for g in range(NG):
                        cols = slice(g * 512, g * 512 + 512)
                        dve.wait_ge(z_ready, n * (DC * NG) + c * NG + g + 1)
                        nc.vector.tensor_tensor(yg[:, c, cols], yg[:, c, cols], zs[:, c, cols],
                                                ALU.mult).then_inc(yg_ready, 1)
                for j in range(NT):
                    u = U_OUT + j
                    full(dve, n, u)
                    nc.vector.tensor_tensor(x1[:, j, :], xn[:, j, :], mm[:, u % 2, 0:DM], ALU.add).then_inc(mm_free[u % 2], 1)
                for u in (U_OUT + NT - 2, U_OUT + NT - 1):
                    read_out(dve, n, u)
                for j in range(NT):
                    last = nc.vector.bn_stats(st[:, j, :], x1[:, j, :])
                last.then_inc(rms, 1)
                dve.wait_ge(rms, n * 6 + 1)
                apart(dve)
                for j in range(NT):
                    last = nc.vector.bn_aggr(mv[:, j, :], st[:, j, :])
                last.then_inc(rms, 1)
                dve.wait_ge(rms, n * 6 + 2)
                nc.vector.tensor_tensor(ms[:, :], mv[:, :, 0], mv[:, :, 0], ALU.mult).then_inc(rms, 1)
                dve.wait_ge(rms, n * 6 + 3)
                nc.vector.tensor_tensor(ms[:, :], ms[:, :], mv[:, :, 1], ALU.add).then_inc(rms, 1)
                dve.wait_ge(rms, n * 6 + 4)
                nc.vector.tensor_scalar(ms[:, :], ms[:, :], RMS_EPS, None, ALU.add).then_inc(rms, 1)
                dve.wait_ge(rms, n * 6 + 5)
                nc.vector.reciprocal(rr, ms[:, :]).then_inc(rms, 1)
                dve.wait_ge(rooted, n * 2 + 2)
                for j in range(NT):
                    nc.vector.tensor_scalar(x1r[:, j, :], x1[:, j, :], roots[:, 1, j:j + 1], None, ALU.mult).then_inc(x1r_ready, 1)
                dve.wait_ge(gated, n + 1)
                dve.wait_ge(x_again, n * 16 + 16)
                for q in range(NQ):
                    u = U_MLP + q * PER_Q + HC // 2
                    t = slice(2 * q, 2 * q + 2)
                    full(dve, n, u)
                    nc.vector.tensor_tensor(x1[:, t, :], x1[:, t, :], mm[:, u % 2, :].rearrange("p (t d) -> p t d", t=2),
                                            ALU.add).then_inc(mm_free[u % 2], 1)
                    read_out(dve, n, u)
                    nc.vector.tensor_tensor(res[:, t, :], x1[:, t, :], moe[:, t, :], ALU.mult).then_inc(prod, 1)
                    dve.wait_ge(prod, n * NQ + q + 1)
                    nc.vector.tensor_tensor(res[:, t, :], res[:, t, :], x_sb[:, t, :], ALU.add).then_inc(res_ready, 1)

            with dve.Fori(0, BATCH) as b:
                nc.vector.memset(halo[:, :, :], 0.0).then_inc(reset, 1)
                nc.vector.memset(carry[:, :], 0.0).then_inc(reset, 1)
                dve.wait_ge(reset, b * 2 + 2)
                apart(dve)
                with dve.Fori(0, HALVES) as half:
                    n = b * HALVES + half
                    if True:
                        dve.wait_ge(x_in, n * 16 + 16)
                        nc.vector.tensor_copy(xpad[:, :, 0:TAPS - 1], halo[:, :, :]).then_inc(halo_in, 1)
                    a_block(n)
                    step(n, 0, 0, 0, True, False)
                    with dve.Fori(0, NS // 2 - 1) as i:
                        step(n, i * 2 + 1, 1, i, True, True)
                        step(n, i * 2 + 2, 0, i + 1, True, True)
                    step(n, NS - 1, 1, NE - 1, True, True)
                    step(n, NS, 0, None, False, True)
                    dve.wait_ge(carried, n * NS + NS)
                    c_block(n)


def kernel(**inputs):
    import numpy as np
    import concourse.bacc as bacc
    from concourse.bass_utils import run_bass_kernel_spmd

    def a(name):
        return np.asarray(inputs[name])

    def rows(m):
        k = m.shape[0] // P
        return m.reshape(k, P, -1).transpose(1, 0, 2).reshape(P, -1)

    arrays = {
        "x": a("L0_attn_x").reshape(BATCH * SEQ, DM),
        "params": np.concatenate([
            rows(a("L0_attn_conv_w")), rows(a("L0_attn_conv_b").reshape(DI, 1)), rows(a("L0_attn_dt_proj_b").reshape(DI, 1)),
            rows(a("L0_attn_D").reshape(DI, 1)), a("L0_attn_A_log").reshape(DC, P, NS).transpose(1, 2, 0).reshape(P, -1),
            rows(a("L0_ffn_gate_w")), rows(a("L0_attn_x_proj_w").T)], axis=1),
        "weights": np.concatenate([rows(a("L0_attn_in_proj_w").T), rows(a("L0_attn_out_proj_w").T)], axis=1),
        "w_dt": a("L0_attn_dt_proj_w").T,
        "moe1": np.stack([np.concatenate([rows(a("L0_ffn_w1")[e]), rows(a("L0_ffn_b1")[e].reshape(HID, 1))], axis=1)
                          for e in range(NE)]),
        "moe2": np.stack([rows(a("L0_ffn_w2")[e]) for e in range(NE)]),
        "moe_b2": a("L0_ffn_b2"),
        "gate_b": a("L0_ffn_gate_b"),
        "mlp1": rows(a("L0_attn_mlp_w1").T),
        "mlp2": rows(a("L0_attn_mlp_w2").T),
    }
    arrays = {k: np.ascontiguousarray(v) for k, v in arrays.items()}
    nc = bacc.Bacc("TRN2", target_bir_lowering=False, num_devices=1)
    args = [nc.dram_tensor(k, v.shape, F32, kind="ExternalInput").ap() for k, v in arrays.items()]
    out = nc.dram_tensor("out", (BATCH * SEQ, DM), F32, kind="ExternalOutput").ap()
    b_rows = nc.dram_tensor("b_rows", (BATCH * HALVES * NS, BT), F32, kind="Internal").ap()
    mamba_moe(nc, *args, out, b_rows)
    r = run_bass_kernel_spmd(nc, [arrays], core_ids=[0])
    return r.results[0]["out"].reshape(BATCH, SEQ, DM)
```

```python
from contextlib import ExitStack

import concourse.bass as bass
from concourse import mybir

F32 = mybir.dt.float32
I32 = mybir.dt.int32
ALU = mybir.AluOpType
ACT = mybir.ActivationFunctionType
AX_X = mybir.AxisListType.X

P = 128
BATCH, SEQ, DM = 2, 2048, 256
DI = 2 * DM
NS = 16
RK = 16
XD = RK + 2 * NS
TAPS = 4
NE, HID = 8, 1024
BT = 512
NB = BATCH * SEQ // BT
NT = BT // P
AT = NB * NT
KC = DM // P
DC = DI // P
HC = HID // P
SLOTS = 256
TILES = (2 * BATCH * SEQ + NE * (SLOTS - 1)) // SLOTS
ZTILES = TILES + 1
LN_EPS = 1e-5
RMS_EPS = 1.1920929e-07

P_CONVW = 0
P_CONVB = P_CONVW + DC * TAPS
P_DTB = P_CONVB + DC
P_D = P_DTB + DC
P_ALOG = P_D + DC
P_GATE = P_ALOG + NS * DC
P_XPROJ = P_GATE + KC * NE
P_END = P_XPROJ + DC * XD
W1_COLS = KC * HID + HC

A_USES = ["TR0", "TR1", "IN0", "IN1", "IN2", "IN3", "XD", "CT", "DT0", "DT1", "DT2", "DT3"]
C_USES = (["YT%d" % c for c in range(DC)] + ["Z%d" % c for c in range(DC)] + ["OUT0", "OUT1", "T10", "T11"]
          + [w % q for q in range(2) for w in ("M1%d0", "M1%d1", "M1%d2", "M1%d3", "M2%d0", "M2%d1")])
M_USES = ["UP0", "UP1", "UP2", "UP3", "MT", "DN0", "DN1"]
PRE_AC = NB * KC
PRE_M = 4
PER_BODY = 6
FIRST_BODY = 1
assert PER_BODY * (NB - 1 - FIRST_BODY) < TILES <= PER_BODY * (NB - FIRST_BODY)
assert PRE_AC % 2 == 0 and len(A_USES) % 2 == 0 and len(C_USES) % 2 == 0 and PER_BODY * len(M_USES) % 2 == 0

A_WORK = (["LOADX", "XR", "TR0", "TR1", "HALO", "IN0", "IN1", "IN2", "CV0", "IN3", "SL0", "CV1", "SL1", "CV2",
           "SL2", "CV3", "SL3", "HKEEP", "XD", "BOUT", "CT", "DT0", "DT1", "DT2", "DT3", "SP", "DT", "DTU"])
C_WORK = (["LOADN"] + ["YT%d" % c for c in range(DC)] + ["Z%d" % c for c in range(DC)]
          + ["OUT0", "OUT1", "RMS", "NORM", "T10", "T11"]
          + [w % q for q in range(2) for w in ("M1%d0", "M1%d1", "M1%d2", "M1%d3", "M2%d0", "M2%d1")] + ["STORE"])
M_WORK = ["UP0", "UP1", "UP2", "UP3", "MT", "DN0", "DN1", "NEXT"]


def spread(work, first, last):
    slots = {}
    for i, w in enumerate(work):
        slots.setdefault(first + i * (last - first) // len(work), []).append(w)
    return slots


def schedule(with_c, with_a, tiles):
    n = NS * DC
    c = spread(C_WORK, 5, 42) if with_c else {}
    a = spread(A_WORK, 38, n - 1) if with_a else {}
    m = spread([(w, t) for t in range(tiles) for w in M_WORK], 0, n)
    order = []
    for s in range(NS):
        for k in range(DC):
            i = s * DC + k
            order.append(("S", "SCAN", (s, k)))
            order.append(("Y", "ADD", (s - 1, k)))
            order += [("M", w, t) for w, t in m.get(i, [])]
            order += [("C", w, None) for w in c.get(i, [])]
            order += [("A", w, None) for w in a.get(i, [])]
        order.append(("S", "KEEP", (s, None)))
    return order


def mamba_moe(nc, x, params, weights, w_dt, moe1, moe2, moe_b2, gate_b, mlp, out, b_rows, xn_rows, s_rows,
              slot_x, slot_y):
    with ExitStack() as ctx:
        def sb(name, shape, dtype=F32):
            return ctx.enter_context(nc.sbuf_tensor(name, shape, dtype))

        def sem(name):
            return ctx.enter_context(nc.semaphore(name))

        par = sb("par", [P, P_END])
        wts = sb("wts", [P, KC * 2 * DI + DC * DM])
        w_in = wts[:, 0:KC * 2 * DI].rearrange("p (k n) -> p k n", k=KC)
        w_out = wts[:, KC * 2 * DI:].rearrange("p (k n) -> p k n", k=DC)
        wdt = sb("wdt", [RK, DI])
        wm = sb("wm", [P, KC * HID + HC * DM])
        wm1 = wm[:, 0:KC * HID].rearrange("p (k n) -> p k n", k=KC)
        wm2 = wm[:, KC * HID:].rearrange("p (k n) -> p k n", k=HC)
        ident = sb("ident", [P, P])
        ones = sb("ones", [P, P])
        below = sb("below", [P, P])
        w1 = sb("w1", [P, W1_COLS])
        w1v = w1[:, 0:KC * HID].rearrange("p (k n) -> p k n", k=KC)
        w2 = sb("w2", [P, HC, DM])
        b2row = sb("b2row", [1, DM])
        xs = sb("xs", [P, 2, 2, DM])
        xsT = sb("xsT", [P, KC, SLOTS])
        ys = sb("ys", [P, 2, 2, DM])
        late = sb("late", [P, AT * DM])
        xn_all = late[:, :].rearrange("p (t d) -> p t d", t=AT)
        acc = late[:, 0:2 * NT * DI].rearrange("p (b t d) -> p b t d", b=2, t=NT)
        hid = late[:, 2 * NT * DI:2 * NT * DI + 2 * HC * SLOTS].rearrange("p (b k t) -> p b k t", b=2, k=HC)
        xa = sb("xa", [P, NT, DM])
        x1 = sb("x1", [P, NT, DM])
        xrT = sb("xrT", [P, 2, KC, BT])
        xpad = sb("xpad", [P, DC, TAPS - 1 + BT])
        x1T = xpad[:, 0:KC, 0:BT]
        xc = sb("xc", [P, 2, DC, BT])
        dt = sb("dt", [P, 2, DC, BT])
        dtu = sb("dtu", [P, 2, DC, BT])
        xdT = sb("xdT", [XD, BT])
        xdt = sb("xdt", [P, 2, NT, XD])
        th = sb("th", [P, 2, BT])
        halo = sb("halo", [P, 2, DC, TAPS - 1])
        carry = sb("carry", [P, 2, NS * DC])
        h = sb("h", [P, 2, DC, BT])
        bb = sb("bb", [P, 2, BT])
        dbu = sb("dbu", [P, 2, BT])
        st = sb("st", [P, AT, 6])
        cst = sb("cst", [P, NT, 6])
        mv = sb("mv", [P, AT, 2])
        roots = sb("roots", [P, 2, AT])
        ms = sb("ms", [P, AT])
        cmv = sb("cmv", [P, NT, 2])
        cms = sb("cms", [P, NT])
        croot = sb("croot", [P, NT])
        slots = sb("slots", [P, 2, AT], I32)
        gates = sb("gates", [P, 2, AT])
        eid = sb("eid", [P, ZTILES], I32)
        h_flat = h[:, :, :, :].rearrange("p b c t -> p (b c t)")
        cmp = h_flat[:, 0:AT * NE * NE]
        tie = h_flat[:, AT * NE * NE:2 * AT * NE * NE]
        bb_flat = bb[:, :, :].rearrange("p b t -> p (b t)")
        dbu_flat = dbu[:, :, :].rearrange("p b t -> p (b t)")
        th_flat = th[:, :, :].rearrange("p b t -> p (b t)")
        AE = AT * NE
        lg, prob, rank, sel = (bb_flat[:, i * AE:(i + 1) * AE] for i in range(4))
        m0, m1, tot, incl = (dbu_flat[:, i * AE:(i + 1) * AE] for i in range(4))
        slotf, seg = (th_flat[:, i * AE:(i + 1) * AE] for i in range(2))
        x1_flat = x1[:, :, :].rearrange("p t d -> p (t d)")
        EARLY, GATEB, RED, CNT, COUNTS, NTILE, ENDS, BASE, STEPS, TI, EF = 0, 64, 72, 104, 112, 240, 248, 256, 264, 280, 328
        earlier = x1_flat[:, EARLY:EARLY + NE * NE]
        gateb = x1_flat[:, GATEB:GATEB + NE]
        red = x1_flat[:, RED:RED + AT]
        cnt = x1_flat[:, COUNTS:COUNTS + NE * 16]
        ntile = x1_flat[:, NTILE:NTILE + NE]
        ends = x1_flat[:, ENDS:ENDS + NE]
        base_ = x1_flat[:, BASE:BASE + NE]
        steps = x1_flat[:, STEPS:STEPS + 16]
        ti = x1_flat[:, TI:TI + ZTILES]
        ef = x1_flat[:, EF:EF + ZTILES]
        ecmp = x1_flat[:, 384:384 + ZTILES * NE]
        zeros = dtu[:, :, :, :].rearrange("p b c t -> p (b c t)")[:, 0:2048]
        gy = dt[:, :, :, :].rearrange("p b c t -> p (b c t)").rearrange("p (b k t d) -> p b k t d", b=2, k=2, t=NT)
        sx = dtu[:, :, :, :].rearrange("p b c t -> p (b c t)").rearrange("p (b k t d) -> p b k t d", b=2, k=2, t=NT)

        decay = ctx.enter_context(nc.psum_tensor("decay", [P, 2, BT], F32))
        hT = ctx.enter_context(nc.psum_tensor("hT", [P, 2, DI], F32))
        ac = ctx.enter_context(nc.psum_tensor("ac", [P, 2, 512], F32))
        mo = ctx.enter_context(nc.psum_tensor("mo", [P, 2, 512], F32))

        params_in = sem("params_in")
        wm_in = sem("wm_in")
        consts = sem("consts")
        aside = sem("aside")
        ac_full = [sem("ac_full0"), sem("ac_full1")]
        ac_free = [sem("ac_free0"), sem("ac_free1")]
        mo_full = [sem("mo_full0"), sem("mo_full1")]
        mo_free = [sem("mo_free0"), sem("mo_free1")]
        x_in = [sem("x_in%d" % g) for g in range(NB)]
        neg_a_ready = sem("neg_a_ready")
        halved = sem("halved")
        stats = sem("stats")
        ln_root = sem("ln_root")
        xn_ready = sem("xn_ready")
        xn_out = sem("xn_out")
        zero_out = sem("zero_out")
        router = sem("router")
        router_exp = sem("router_exp")
        routed = sem("routed")
        scattered = sem("scattered")
        xa_in = sem("xa_in")
        xr_ready = sem("xr_ready")
        halo_in = sem("halo_in")
        conv = sem("conv")
        tanh_c = sem("tanh_c")
        xc_ready = sem("xc_ready")
        halo_kept = sem("halo_kept")
        b_out = sem("b_out")
        softplus = sem("softplus")
        ln_done = sem("ln_done")
        dt_ready = sem("dt_ready")
        dtu_ready = sem("dtu_ready")
        bb_in = [sem("bb_in0"), sem("bb_in1")]
        decay_ready = sem("decay_ready")
        dbu_ready = sem("dbu_ready")
        scanned = sem("scanned")
        carried = sem("carried")
        hT_ready = sem("hT_ready")
        y_added = sem("y_added")
        x1_in = sem("x1_in")
        y_skip = sem("y_skip")
        z_tanh = sem("z_tanh")
        z_silu = sem("z_silu")
        rms = sem("rms")
        c_root = sem("c_root")
        x1r_ready = sem("x1r_ready")
        m_tanh = sem("m_tanh")
        s_out = sem("s_out")
        w1_in = sem("w1_in")
        w2_in = sem("w2_in")
        xs_in = [sem("xs_in0"), sem("xs_in1")]
        ys_out = [sem("ys_out0"), sem("ys_out1")]
        gathered = [sem("gathered0"), sem("gathered1")]
        sx_in = [sem("sx_in0"), sem("sx_in1")]
        d_scaled = sem("d_scaled")
        d_mixed = sem("d_mixed")
        d_gate = sem("d_gate")
        d_prod = sem("d_prod")
        d_ready = sem("d_ready")
        stored = [sem("stored0"), sem("stored1")]

        x_t = x.rearrange("(b h t p) d -> h b p t d", b=BATCH, t=NT, p=P)
        out_t = out.rearrange("(b h t p) d -> h b p t d", b=BATCH, t=NT, p=P)
        xn_t = xn_rows.rearrange("(m p t) d -> m p (t d)", p=P, t=NT)
        s_t = s_rows.rearrange("(m p t) d -> m p (t d)", p=P, t=NT)
        slot_x_t = slot_x.rearrange("(i p r) d -> i p (r d)", p=P, r=2)
        slot_y_t = slot_y.rearrange("(i p r) d -> i p (r d)", p=P, r=2)

        def flat3(ap):
            return ap.rearrange("p t d -> p (t d)")

        def before_a(m):
            if isinstance(m, int) and m == 0:
                return PRE_AC // 2
            return m * ((len(A_USES) + len(C_USES)) // 2) + (PRE_AC - len(C_USES)) // 2

        def before_c(m):
            last = isinstance(m, int) and m == NB - 1
            a_uses = NB * len(A_USES) // 2 if last else (m + 2) * (len(A_USES) // 2)
            return a_uses + m * (len(C_USES) // 2) + PRE_AC // 2

        def before_m(n):
            return (n - FIRST_BODY) * (PER_BODY * len(M_USES) // 2) + PRE_M // 2

        def full(eng, sems, before, u):
            eng.wait_ge(sems[u % 2], before + (u // 2 + 1))

        def free(eng, sems, before, u):
            eng.wait_ge(sems[u % 2], before + (u // 2 + 1))

        def read_out(eng, sems, before, u):
            eng.wait_ge(sems[u % 2], before + (u // 2 + 2))

        def apart(eng):
            eng.sem_inc(aside, 1)

        def walk(eng, do):
            def body(n, p, with_c, with_a, tiles):
                for kind, name, i in schedule(with_c, with_a, tiles):
                    if kind == "S":
                        do(kind, name, i, n, p)
                    elif kind == "Y" and i[0] >= 0:
                        do(kind, name, i, n, p)
                    elif kind == "Y" and with_c:
                        do(kind, name, (NS - 1, i[1]), n - 1, 1 - p)
                    elif kind == "C":
                        do(kind, name, i, n - 1, 1 - p)
                    elif kind == "A":
                        do(kind, name, i, n + 1, 1 - p)
                    elif kind == "M":
                        do(kind, name, i, n, p)

            for name in A_WORK:
                do("A", name, None, 0, 0)
            body(0, 0, False, True, 0)
            do("M", "START", None, 0, 0)
            with eng.Fori(0, (NB - 2) // 2) as i:
                body(i * 2 + 1, 1, True, True, PER_BODY)
                body(i * 2 + 2, 0, True, True, PER_BODY)
            body(NB - 1, 1, True, False, TILES - PER_BODY * (NB - 1 - FIRST_BODY))
            for k in range(DC):
                do("Y", "ADD", (NS - 1, k), NB - 1, 1)
            for name in C_WORK:
                do("C", name, None, NB - 1, 1)

        CONSTS = 14
        STATS = 2 * NB + 5
        AE = AT * NE
        neg_a = par[:, P_ALOG:P_ALOG + NS * DC]

        def x_dst(g):
            return xn_all[:, g * NT:(g + 1) * NT, :]

        def is_last_tile(m, i):
            return int(isinstance(m, int) and (m - FIRST_BODY) * PER_BODY + i == TILES - 1)

        def store(sp, g):
            sp.wait_ge(d_ready, g + 1)
            sp.dma_start(out_t[g // 2, g % 2], sx[:, g % 2, 0]).then_inc(stored[g % 2], 16)

        def finish(dve, g):
            b = g % 2
            dve.wait_ge(d_gate, g + 1)
            dve.wait_ge(sx_in[b], 32 * (g // 2 + 1))
            nc.vector.tensor_tensor(sx[:, b, 0], sx[:, b, 0], gy[:, b, 0], ALU.mult).then_inc(d_prod, 1)
            dve.wait_ge(d_prod, g + 1)
            nc.vector.tensor_tensor(sx[:, b, 0], sx[:, b, 0], sx[:, b, 1], ALU.add).then_inc(d_ready, 1)

        block = ctx.enter_context(nc.Block())

        @block.sync
        def _(sp):
            sp.dma_start(x_dst(0), x_t[0, 0]).then_inc(x_in[0], 16)
            sp.dma_start(par[:, :], params).then_inc(params_in, 16)
            for g in range(1, NB):
                sp.dma_start(x_dst(g), x_t[g // 2, g % 2]).then_inc(x_in[g], 16)
            sp.dma_start(gateb, gate_b.partition_broadcast(P)).then_inc(params_in, 16)
            sp.dma_start(wts[:, :], weights).then_inc(params_in, 16)
            sp.dma_start(wdt[:, :], w_dt).then_inc(params_in, 16)
            sp.dma_start(wm[:, :], mlp).then_inc(wm_in, 16)
            sp.wait_ge(consts, CONSTS)
            rows = 2048 // DM * P
            for i in range(ZTILES * SLOTS // rows):
                sp.dma_start(slot_x[i * rows:(i + 1) * rows, :].rearrange("(p t) d -> p (t d)", p=P),
                             zeros).then_inc(zero_out, 16)
            for g in range(NB):
                sp.wait_ge(xn_ready, g * NT + NT)
                sp.dma_start(xn_t[g], flat3(xn_all[:, g * NT:(g + 1) * NT, :])).then_inc(xn_out, 16)
            sp.wait_ge(xn_out, 16 * NB)

            def load_first(i):
                apart(sp)
                e = sp.value_load(eid[0:1, bass.ds(i, 1)], min_val=0, max_val=NE - 1)
                sp.dma_start(w1[:, :], moe1[bass.ds(e, 1)].rearrange("a p n -> p (a n)")).then_inc(w1_in, 16)

            def load_second(i):
                apart(sp)
                e = sp.value_load(eid[0:1, bass.ds(i, 1)], min_val=0, max_val=NE - 1)
                sp.dma_start(w2[:, :, :].rearrange("p k n -> p (k n)"),
                             moe2[bass.ds(e, 1)].rearrange("a p n -> p (a n)")).then_inc(w2_in, 16)
                sp.dma_start(b2row[:, :], moe_b2[bass.ds(e, 1)]).then_inc(w2_in, 16)

            def load_rows(i, slot):
                sp.dma_start(xs[:, slot, :, :].rearrange("p r d -> p (r d)"),
                             slot_x_t[bass.ds(i, 1)].rearrange("a p n -> p (a n)")).then_inc(xs_in[slot], 16)

            def load_b(m, s):
                sp.dma_start(bb[:, s % 2, :], b_rows[bass.ds(m * NS + s, 1), :].rearrange("a t -> (a t)")
                             .partition_broadcast(P)).then_inc(bb_in[s % 2], 16)

            def do(kind, name, i, m, p):
                if kind == "S" and name == "SCAN" and i[1] == 0:
                    s = i[0]
                    if s == 0:
                        sp.wait_ge(b_out, m * 16 + 16)
                        apart(sp)
                        if not (isinstance(m, int) and m == 0):
                            sp.wait_ge(dbu_ready, m * (NS * DC))
                        else:
                            sp.wait_ge(routed, 2)
                        load_b(m, 0)
                        load_b(m, 1)
                    elif s < NS - 1:
                        sp.wait_ge(dbu_ready, m * (NS * DC) + s * DC)
                        load_b(m, s + 1)
                elif kind == "A" and name == "LOADX":
                    if isinstance(m, int) and m == 1:
                        full(sp, ac_full, before_a(0), A_USES.index("TR1"))
                    elif not isinstance(m, int):
                        full(sp, ac_full, before_c(m - 2), C_USES.index("T11"))
                    sp.dma_start(flat3(xa[:, :, :]), xn_t[bass.ds(m, 1)].rearrange("a p n -> p (a n)")).then_inc(xa_in, 16)
                elif kind == "C" and name == "LOADN":
                    sp.wait_ge(s_out, m * 16 + 16)
                    if isinstance(m, int) is False or m == 0:
                        sp.wait_ge(routed, 2)
                    sp.dma_start(flat3(x1[:, :, :]), xn_t[bass.ds(m, 1)].rearrange("a p n -> p (a n)")).then_inc(x1_in, 16)
                elif kind == "C" and name == "STORE":
                    read_out(sp, ac_free, before_c(m), C_USES.index("M210"))
                    read_out(sp, ac_free, before_c(m), C_USES.index("M211"))
                    sp.dma_start(s_t[bass.ds(m, 1)].rearrange("a p n -> p (a n)"), flat3(x1[:, :, :])).then_inc(s_out, 16)
                elif kind == "M":
                    if name == "START":
                        sp.wait_ge(scattered, 16 * 2 * AT)
                        load_first(0)
                        load_rows(0, 0)
                        load_second(0)
                        load_rows(1, 1)
                        return
                    tile = (m - FIRST_BODY) * PER_BODY + i
                    last = isinstance(m, int) and tile == TILES - 1
                    if name == "MT" and not last:
                        read_out(sp, mo_free, before_m(m), i * len(M_USES) + M_USES.index("UP3"))
                        load_first(tile + 1)
                    elif name == "NEXT" and not last:
                        full(sp, mo_full, before_m(m), i * len(M_USES) + M_USES.index("DN1"))
                        load_second(tile + 1)
                        if not (isinstance(m, int) and tile == TILES - 2):
                            load_rows(tile + 2, i % 2)

            walk(sp, do)
            for g in range(NB):
                if g == 0:
                    sp.wait_ge(scanned, NB * NS * DC + 2)
                    sp.wait_ge(s_out, 16 + 16 * (NB - 1))
                if g == NB - 1:
                    sp.wait_ge(s_out, 16 + 16 * NB)
                if g >= 2:
                    sp.wait_ge(stored[g % 2], 16 * (g // 2))
                sp.dma_start(flat3(sx[:, g % 2, 0]), s_t[g]).then_inc(sx_in[g % 2], 16)
                sp.dma_start(sx[:, g % 2, 1], x_t[g // 2, g % 2]).then_inc(sx_in[g % 2], 16)
                if g >= 1:
                    store(sp, g - 1)
            store(sp, NB - 1)
            for b in range(2):
                sp.wait_ge(stored[b], 16 * NB // 2)
                sp.wait_ge(ys_out[b], 16 * ((TILES + 1 - b) // 2) + 16)

        @block.gpsimd
        def _(pool):
            def iota(dst, pattern, cm=0):
                nc.gpsimd.iota(dst, pattern, base=0, channel_multiplier=cm,
                               allow_small_or_imprecise_dtypes=True).then_inc(consts, 1)
            nc.gpsimd.memset(ident[:, :], 0.0).then_inc(consts, 1)
            nc.gpsimd.memset(below[:, :], 0.0).then_inc(consts, 1)
            nc.gpsimd.memset(earlier, 0.0).then_inc(consts, 1)
            nc.gpsimd.memset(seg, 1.0).then_inc(consts, 1)
            pool.wait_ge(consts, 4)
            nc.gpsimd.affine_select(out=ident[:, :], in_=ident[:, :], compare_op=ALU.not_equal, fill=1.0,
                                    base=0, pattern=[[-1, P]], channel_multiplier=1).then_inc(consts, 1)
            nc.gpsimd.affine_select(out=below[:, :], in_=below[:, :], compare_op=ALU.is_ge, fill=1.0,
                                    base=0, pattern=[[-1, P]], channel_multiplier=1).then_inc(consts, 1)
            e3 = earlier.rearrange("p (e f) -> p e f", e=NE)
            nc.gpsimd.affine_select(out=e3, in_=e3, compare_op=ALU.is_ge, fill=1.0,
                                    base=0, pattern=[[-1, NE], [1, NE]], channel_multiplier=0).then_inc(consts, 1)
            nc.gpsimd.memset(seg.rearrange("p (e t) -> p e t", e=NE)[:, :, 0:1], 0.0).then_inc(consts, 1)
            nc.gpsimd.memset(ones[:, :], 1.0).then_inc(consts, 1)
            nc.gpsimd.memset(zeros, 0.0).then_inc(consts, 1)
            iota(steps, [[SLOTS, 16]])
            iota(ti, [[1, ZTILES]])
            nc.gpsimd.memset(halo[:, :, :, :], 0.0).then_inc(consts, 1)
            nc.gpsimd.memset(carry[:, :, :], 0.0).then_inc(consts, 1)

            def scatter(j):
                for k in range(2):
                    pool.indirect_dma_start(
                        out=slot_x, out_offset=bass.IndirectOffsetOnAxis(ap=slots[:, k, j:j + 1], axis=0),
                        in_=xn_all[:, j, :], in_offset=None).then_inc(scattered, 16)

            def do(kind, name, i, m, p):
                if kind == "S" and name == "SCAN":
                    s, c = i
                    first = isinstance(m, int) and m == 0
                    if first and s == 0 and c == 0:
                        pool.wait_ge(routed, 2)
                        pool.wait_ge(zero_out, 16 * (ZTILES * SLOTS * DM // (2048 * P)))
                        for j in range(AT):
                            scatter(j)
                    if s == 0 and c == 0:
                        pool.wait_ge(dtu_ready, m + 1)
                    if c == 0:
                        pool.wait_ge(bb_in[s % 2], m * (NS * 8) + (s // 2 * 16 + 16))
                    pool.wait_ge(scanned, m * (NS * DC) + (s * DC + c + 1))
                    nc.gpsimd.tensor_tensor(dbu[:, c % 2, :], dtu[:, p, c, :], bb[:, s % 2, :],
                                            ALU.mult).then_inc(dbu_ready, 1)

            walk(pool, do)
            for g in range(NB):
                if g == 0:
                    pool.wait_ge(scanned, NB * NS * DC + 2)
                    for b in range(2):
                        pool.wait_ge(ys_out[b], 16 * ((TILES + 1 - b) // 2) + 16)
                if g >= 2:
                    pool.wait_ge(d_prod, g - 1)
                for t in range(NT):
                    for k in range(2):
                        pool.indirect_dma_start(
                            out=gy[:, g % 2, k, t, :], out_offset=None, in_=slot_y,
                            in_offset=bass.IndirectOffsetOnAxis(ap=slots[:, k, g * NT + t:g * NT + t + 1], axis=0)
                        ).then_inc(gathered[g % 2], 16)

        @block.scalar
        def _(act):
            act.wait_ge(params_in, 64)
            nc.scalar.activation(neg_a, neg_a, ACT.Exp).then_inc(neg_a_ready, 1)
            act.wait_ge(neg_a_ready, 1)
            nc.scalar.mul(neg_a, neg_a, -1.0).then_inc(neg_a_ready, 1)
            act.wait_ge(stats, STATS)
            nc.scalar.activation(roots[:, :, :], roots[:, :, :], ACT.Sqrt).then_inc(ln_root, 1)
            for g in range(NB):
                for k in range(KC):
                    u = g * KC + k
                    full(act, ac_full, 0, u)
                    nc.scalar.copy(xrT[:, g % 2, k, :], ac[:, u % 2, :]).then_inc(ac_free[u % 2], 1)
            act.wait_ge(router, 3)
            nc.scalar.activation(lg, lg, ACT.Exp).then_inc(router_exp, 1)

            def do(kind, name, i, m, p):
                if kind == "S" and name == "SCAN":
                    s, c = i
                    if s == 0 and c == 0:
                        act.wait_ge(dt_ready, m + 1)
                        act.wait_ge(neg_a_ready, 2)
                    act.wait_ge(scanned, m * (NS * DC) + (s * DC + c + 1))
                    nc.scalar.activation(decay[:, c % 2, :], dt[:, p, c, :], ACT.Exp,
                                         scale=par[:, P_ALOG + s * DC + c:P_ALOG + s * DC + c + 1]).then_inc(decay_ready, 1)
                elif kind == "A":
                    b = before_a(m)
                    if name[:2] == "TR":
                        k = int(name[2])
                        u = A_USES.index(name)
                        full(act, ac_full, b, u)
                        nc.scalar.copy(xrT[:, p, k, :], ac[:, u % 2, :]).then_inc(ac_free[u % 2], 1)
                    elif name[:2] == "IN":
                        c = int(name[2])
                        u = A_USES.index(name)
                        full(act, ac_full, b, u)
                        nc.scalar.copy(xpad[:, c, TAPS - 1:], ac[:, u % 2, :]).then_inc(ac_free[u % 2], 1)
                    elif name[:2] == "CV":
                        c = int(name[2])
                        act.wait_ge(conv, m * (DC * TAPS) + (c + 1) * TAPS)
                        nc.scalar.activation(dtu[:, p, c, :], xc[:, p, c, :], ACT.Tanh).then_inc(tanh_c, 1)
                    elif name == "XD":
                        u = A_USES.index(name)
                        if not (isinstance(m, int) and m == 0):
                            act.wait_ge(b_out, m * 16)
                        full(act, ac_full, b, u)
                        nc.scalar.copy(xdT[:, :], ac[0:XD, u % 2, :]).then_inc(ac_free[u % 2], 1)
                    elif name == "BOUT":
                        read_out(act, ac_free, b, A_USES.index("XD"))
                        act.dma_start(b_rows[bass.ds(m * NS, NS), :], xdT[RK:RK + NS, :]).then_inc(b_out, 16)
                    elif name[:2] == "DT" and len(name) == 3 and name[2] != "U":
                        c = int(name[2])
                        u = A_USES.index(name)
                        full(act, ac_full, b, u)
                        bias = par[:, P_DTB + c:P_DTB + c + 1]
                        nc.scalar.activation(dt[:, p, c, :], ac[:, u % 2, :], ACT.Abs, bias=bias).then_inc(softplus, 1)
                        nc.scalar.activation(dtu[:, p, c, :], ac[:, u % 2, :], ACT.Relu,
                                             bias=bias).then_inc(ac_free[u % 2], 1)
                    elif name == "SP":
                        act.wait_ge(softplus, m * (DC + 1) + DC)
                        nc.scalar.activation(dt[:, p, :, :], dt[:, p, :, :], ACT.Exp, scale=-1.0).then_inc(softplus, 1)
                        act.wait_ge(softplus, m * (DC + 1) + (DC + 1))
                        nc.scalar.activation(dt[:, p, :, :], dt[:, p, :, :], ACT.Ln, bias=1.0).then_inc(ln_done, 1)
                elif kind == "C":
                    b = before_c(m)
                    if name[0] == "Z":
                        u = C_USES.index(name)
                        full(act, ac_full, b, u)
                        nc.scalar.activation(th[:, u % 2, :], ac[:, u % 2, :], ACT.Tanh, scale=0.5).then_inc(z_tanh, 1)
                    elif name == "RMS":
                        act.wait_ge(rms, m * 6 + 6)
                        nc.scalar.activation(croot[:, :], croot[:, :], ACT.Sqrt).then_inc(c_root, 1)
                    elif name[:2] == "T1":
                        u = C_USES.index(name)
                        full(act, ac_full, b, u)
                        nc.scalar.copy(x1T[:, int(name[2]), :], ac[:, u % 2, :]).then_inc(ac_free[u % 2], 1)
                    elif name[:2] == "M1":
                        u = C_USES.index(name)
                        full(act, ac_full, b, u)
                        nc.scalar.activation(th[:, u % 2, :], ac[:, u % 2, :], ACT.Tanh, scale=0.5).then_inc(m_tanh, 1)
                elif kind == "M":
                    if name == "START":
                        for r in range(2):
                            full(act, mo_full, 0, 2 + r)
                            nc.scalar.copy(xsT[:, :, r:SLOTS:2], mo[:, r, 0:KC * P].rearrange("p (k t) -> p k t", k=KC)
                                           ).then_inc(mo_free[r], 1)
                        return
                    b = before_m(m)
                    if name[:2] == "UP":
                        pair = int(name[2])
                        u = i * len(M_USES) + M_USES.index(name)
                        full(act, mo_full, b, u)
                        for j in range(2):
                            hc = 2 * pair + j
                            last = nc.scalar.activation(hid[:, 0, hc, :], mo[:, u % 2, j * SLOTS:(j + 1) * SLOTS],
                                                        ACT.Relu, bias=w1[:, KC * HID + hc:KC * HID + hc + 1])
                        last.then_inc(mo_free[u % 2], 1)
                    elif name == "MT":
                        u = i * len(M_USES) + M_USES.index(name)
                        if is_last_tile(m, i):
                            return
                        full(act, mo_full, b, u)
                        nc.scalar.copy(xsT[:, :, :].rearrange("p k (t r) -> p k r t", r=2),
                                       mo[:, u % 2, :].rearrange("p (k r t) -> p k r t", k=KC, r=2)).then_inc(mo_free[u % 2], 1)
                    elif name[:2] == "DN":
                        r = int(name[2])
                        u = i * len(M_USES) + M_USES.index(name) - is_last_tile(m, i)
                        if r == 0:
                            act.wait_ge(ys_out[i % 2], (m - FIRST_BODY) * (16 * PER_BODY // 2) + (i // 2 * 16 + 16))
                        full(act, mo_full, b, u)
                        nc.scalar.copy(ys[:, i % 2, r, :], mo[:, u % 2, 0:DM]).then_inc(mo_free[u % 2], 1)
                        if r == 1:
                            tile = (m - FIRST_BODY) * PER_BODY + i
                            read_out(act, mo_free, b, u)
                            act.dma_start(slot_y_t[bass.ds(tile, 1)].rearrange("a p n -> p (a n)"),
                                          ys[:, i % 2, :, :].rearrange("p r d -> p (r d)")).then_inc(ys_out[i % 2], 16)

            walk(act, do)
            for g in range(NB):
                act.wait_ge(gathered[g % 2], 16 * 2 * NT * (g // 2 + 1))
                for t in range(NT):
                    j = g * NT + t
                    last = nc.scalar.mul(gy[:, g % 2, 0, t, :], gy[:, g % 2, 0, t, :], gates[:, 0, j:j + 1])
                last.then_inc(d_scaled, 1)
                act.wait_ge(d_mixed, g + 1)
                nc.scalar.activation(gy[:, g % 2, 0], gy[:, g % 2, 0], ACT.Silu).then_inc(d_gate, 1)

        @block.tensor
        def _(pe):
            pe.wait_ge(params_in, 64)
            pe.wait_ge(consts, CONSTS)
            for g in range(NB):
                pe.wait_ge(xn_ready, g * NT + NT)
                for k in range(KC):
                    u = g * KC + k
                    free(pe, ac_free, 0, u)
                    for j in range(NT):
                        last = pe.transpose(ac[:, u % 2, j * P:j * P + P], xn_all[:, g * NT + j, k * P:k * P + P], ident[:, :])
                    last.then_inc(ac_full[u % 2], 1)
                for k in range(KC):
                    read_out(pe, ac_free, 0, g * KC + k)
                for j in range(NT):
                    t = g * NT + j
                    for k in range(KC):
                        last = pe.matmul(mo[:, 0, t * NE:t * NE + NE], xrT[:, g % 2, k, j * P:j * P + P],
                                         par[:, P_GATE + k * NE:P_GATE + k * NE + NE], start=(k == 0), stop=(k == KC - 1))
            last.then_inc(mo_full[0], 1)
            pe.wait_ge(router, 12)
            pe.matmul(mo[:, 1, 0:AE], below[:, :], sel, start=True, stop=True)
            pe.matmul(mo[:, 1, AE:2 * AE], ones[:, :], sel, start=True, stop=True).then_inc(mo_full[1], 1)

            def products(dst, lhs, rhs, n):
                for k in range(n):
                    last = pe.matmul(dst, lhs(k), rhs(k), start=(k == 0), stop=(k == n - 1))
                return last

            def transposes(dst, pieces):
                for j, src in enumerate(pieces):
                    last = pe.transpose(dst[:, j * P:j * P + P], src, ident[:, :])
                return last

            def do(kind, name, i, m, p):
                if kind == "Y":
                    s, j = i
                    if j == 0:
                        pe.wait_ge(scanned, m * (NS * DC) + (s * DC + DC + 2))
                    pe.wait_ge(y_added, m * (NS * NT) + (s * NT + j + 1))
                    transposes(hT[:, j % 2, :], [h[:, s % 2, c, j * P:j * P + P] for c in range(DC)]).then_inc(hT_ready, 1)
                elif kind == "A" and name in A_USES:
                    u = A_USES.index(name)
                    b = before_a(m)
                    dst = ac[:, u % 2, :]
                    if name[:2] == "TR":
                        k = int(name[2])
                        if k == 0:
                            pe.wait_ge(xr_ready, m + 1)
                        free(pe, ac_free, b, u)
                        last = transposes(dst, [xa[:, j, k * P:k * P + P] for j in range(NT)])
                    elif name[:2] == "IN":
                        c = int(name[2])
                        if c == 0:
                            read_out(pe, ac_free, b, A_USES.index("TR0"))
                            read_out(pe, ac_free, b, A_USES.index("TR1"))
                        free(pe, ac_free, b, u)
                        last = products(dst, lambda k: w_in[:, k, c * P:c * P + P], lambda k: xrT[:, p, k, :], KC)
                    elif name == "XD":
                        pe.wait_ge(xc_ready, m * DC + DC)
                        free(pe, ac_free, b, u)
                        last = products(dst[0:XD, :], lambda c: par[:, P_XPROJ + c * XD:P_XPROJ + c * XD + XD],
                                        lambda c: xc[:, p, c, :], DC)
                    elif name == "CT":
                        read_out(pe, ac_free, b, A_USES.index("XD"))
                        free(pe, ac_free, b, u)
                        apart(pe)
                        for j in range(NT):
                            last = pe.transpose(dst[:, j * XD:j * XD + XD], xdT[:, j * P:j * P + P], ident[0:XD, 0:XD])
                    else:
                        c = int(name[2])
                        free(pe, ac_free, b, u)
                        last = pe.matmul(dst, wdt[:, c * P:c * P + P], xdT[0:RK, :], start=True, stop=True)
                    last.then_inc(ac_full[u % 2], 1)
                elif kind == "C" and name in C_USES:
                    u = C_USES.index(name)
                    b = before_c(m)
                    dst = ac[:, u % 2, :]
                    if name[:2] == "YT":
                        c = int(name[2])
                        if c == 0:
                            pe.wait_ge(y_added, m * (NS * NT) + (NS * NT + 2))
                        free(pe, ac_free, b, u)
                        last = transposes(dst, [acc[:, p, j, c * P:c * P + P] for j in range(NT)])
                    elif name[0] == "Z":
                        c = int(name[1]) + DC
                        free(pe, ac_free, b, u)
                        last = products(dst, lambda k: w_in[:, k, c * P:c * P + P], lambda k: xrT[:, p, k, :], KC)
                    elif name[:3] == "OUT":
                        if name == "OUT0":
                            read_out(pe, ac_free, b, C_USES.index("Z2"))
                            read_out(pe, ac_free, b, C_USES.index("Z3"))
                        free(pe, ac_free, b, u)
                        for r in range(2):
                            j = 2 * int(name[3]) + r
                            last = products(dst[:, r * DM:r * DM + DM], lambda c: xc[:, p, c, j * P:j * P + P],
                                            lambda c: w_out[:, c, :], DC)
                    elif name[:2] == "T1":
                        k = int(name[2])
                        if k == 0:
                            pe.wait_ge(x1r_ready, m + 1)
                        free(pe, ac_free, b, u)
                        last = transposes(dst, [xa[:, j, k * P:k * P + P] for j in range(NT)])
                    elif name[:2] == "M1":
                        q, pair = int(name[2]), int(name[3])
                        if q == 0 and pair == 0:
                            pe.wait_ge(wm_in, 16)
                            read_out(pe, ac_free, b, C_USES.index("T10"))
                            read_out(pe, ac_free, b, C_USES.index("T11"))
                        free(pe, ac_free, b, u)
                        for r in range(2):
                            hc = 2 * pair + r
                            last = products(dst[:, r * 256:r * 256 + 256], lambda k: wm1[:, k, hc * P:hc * P + P],
                                            lambda k: x1T[:, k, q * 256:q * 256 + 256], KC)
                    else:
                        q, r = int(name[2]), int(name[3])
                        if r == 0:
                            read_out(pe, ac_free, b, C_USES.index("M1%d2" % q))
                            read_out(pe, ac_free, b, C_USES.index("M1%d3" % q))
                        free(pe, ac_free, b, u)
                        last = products(dst[:, 0:DM], lambda k: hid[:, 1, k, r * P:r * P + P], lambda k: wm2[:, k, :], HC)
                    last.then_inc(ac_full[u % 2], 1)
                elif kind == "M":
                    if name == "START":
                        pe.wait_ge(xs_in[0], 16)
                        for r in range(2):
                            free(pe, mo_free, 0, 2 + r)
                            transposes(mo[:, r, :], [xs[:, 0, r, k * P:k * P + P] for k in range(KC)]).then_inc(mo_full[r], 1)
                        return
                    if name == "NEXT":
                        return
                    b = before_m(m)
                    tile = (m - FIRST_BODY) * PER_BODY + i
                    last_tile = is_last_tile(m, i)
                    u = i * len(M_USES) + M_USES.index(name)
                    if name[:2] == "UP":
                        pair = int(name[2])
                        if pair == 0:
                            if i == 0:
                                read_out(pe, mo_free, b, -1)
                                read_out(pe, mo_free, b, -2)
                            else:
                                read_out(pe, mo_free, b, (i - 1) * len(M_USES) + M_USES.index("MT"))
                            pe.wait_ge(w1_in, tile * 16 + 16)
                        free(pe, mo_free, b, u)
                        for r in range(2):
                            hc = 2 * pair + r
                            last = products(mo[:, u % 2, r * SLOTS:(r + 1) * SLOTS], lambda k: w1v[:, k, hc * P:hc * P + P],
                                            lambda k: xsT[:, k, :], KC)
                    elif name == "MT":
                        if last_tile:
                            return
                        pe.wait_ge(xs_in[(i + 1) % 2],
                                   (m - FIRST_BODY) * (16 * PER_BODY // 2) + ((i + 1) // 2 * 16 + 16))
                        free(pe, mo_free, b, u)
                        last = transposes(mo[:, u % 2, :], [xs[:, (i + 1) % 2, r, k * P:k * P + P]
                                                            for k in range(KC) for r in range(2)])
                    else:
                        r = int(name[2])
                        if r == 0:
                            first_u = i * len(M_USES)
                            read_out(pe, mo_free, b, first_u + M_USES.index("UP2"))
                            read_out(pe, mo_free, b, first_u + M_USES.index("UP3"))
                            pe.wait_ge(w2_in, tile * 32 + 32)
                        u -= last_tile
                        free(pe, mo_free, b, u)
                        o = mo[:, u % 2, 0:DM]
                        for k in range(HC):
                            pe.matmul(o, hid[:, 0, k, r:SLOTS:2], w2[:, k, :], start=(k == 0), stop=False)
                        last = pe.matmul(o, ones[0:1, :], b2row[:, :], start=False, stop=True)
                    last.then_inc(mo_full[u % 2], 1)

            walk(pe, do)

        @block.vector
        def _(dve):
            for s_, v in ((ac_free[0], 1), (ac_free[1], 1), (mo_free[0], 1), (mo_free[1], 1), (scanned, 2),
                          (y_added, 2), (s_out, 16), (ys_out[0], 16), (ys_out[1], 16)):
                dve.sem_inc(s_, v)
            dve.wait_ge(params_in, 64)
            dve.wait_ge(consts, CONSTS)
            nc.vector.tensor_scalar(par[:, P_CONVW:P_DTB], par[:, P_CONVW:P_DTB], 0.5, None, ALU.mult).then_inc(halved, 1)

            for g in range(NB):
                dve.wait_ge(x_in[g], 16)
                for t in range(NT):
                    last = nc.vector.bn_stats(st[:, g * NT + t, :], xn_all[:, g * NT + t, :])
                last.then_inc(stats, 1)
                dve.wait_ge(stats, 2 * g + 1)
                for t in range(NT):
                    last = nc.vector.bn_aggr(mv[:, g * NT + t, :], st[:, g * NT + t, :])
                last.then_inc(stats, 1)
            n = 2 * NB
            dve.wait_ge(stats, n)
            nc.vector.tensor_scalar(ms[:, :], mv[:, :, 1], LN_EPS, None, ALU.add).then_inc(stats, 1)
            dve.wait_ge(stats, n + 1)
            nc.vector.reciprocal(roots[:, 0, :], ms[:, :]).then_inc(stats, 1)
            dve.wait_ge(stats, n + 2)
            nc.vector.tensor_tensor(ms[:, :], mv[:, :, 1], roots[:, 0, :], ALU.mult).then_inc(stats, 1)
            dve.wait_ge(stats, n + 3)
            nc.vector.tensor_scalar(ms[:, :], ms[:, :], RMS_EPS, None, ALU.add).then_inc(stats, 1)
            dve.wait_ge(stats, n + 4)
            nc.vector.reciprocal(roots[:, 1, :], ms[:, :]).then_inc(stats, 1)
            dve.wait_ge(ln_root, 1)
            for t in range(AT):
                nc.vector.tensor_scalar(xn_all[:, t, :], xn_all[:, t, :], mv[:, t, 0:1], roots[:, 0, t:t + 1],
                                        ALU.subtract, ALU.mult).then_inc(xn_ready, 1)

            done = [0]

            def step(ins):
                done[0] += 1
                ins.then_inc(router, 1)
                dve.wait_ge(router, done[0])

            def by_te(a):
                return a.rearrange("p (t e) -> p t e", e=NE)

            def over_e(a, n=AT):
                return a.rearrange("p (t a) -> p t a", a=1).broadcast_to([P, n, NE])

            def over_t(a, n=AT):
                return a.rearrange("p (a e) -> p a e", a=1).broadcast_to([P, n, NE])

            full(dve, mo_full, 0, 0)
            step(nc.vector.tensor_tensor(by_te(lg), by_te(mo[:, 0, 0:AE]), over_t(gateb), ALU.add))
            step(nc.vector.tensor_reduce(red, by_te(lg), AX_X, ALU.max))
            step(nc.vector.tensor_tensor(by_te(lg), by_te(lg), over_e(red), ALU.subtract))
            dve.sem_inc(mo_free[0], 1)
            dve.wait_ge(router_exp, 1)
            step(nc.vector.tensor_reduce(red, by_te(lg), AX_X, ALU.add))
            step(nc.vector.reciprocal(red, red))
            step(nc.vector.tensor_tensor(by_te(prob), by_te(lg), over_e(red), ALU.mult))
            c4 = cmp.rearrange("p (t e f) -> p t e f", e=NE, f=NE)
            t4 = tie.rearrange("p (t e f) -> p t e f", e=NE, f=NE)
            this = prob.rearrange("p (t e a) -> p t e a", e=NE, a=1).broadcast_to([P, AT, NE, NE])
            other = prob.rearrange("p (t a e) -> p t a e", e=NE, a=1).broadcast_to([P, AT, NE, NE])
            nc.vector.tensor_tensor(c4, other, this, ALU.is_gt)
            step(nc.vector.tensor_tensor(t4, other, this, ALU.is_equal))
            t3 = tie.rearrange("p (t f) -> p t f", f=NE * NE)
            eb = earlier.rearrange("p (a f) -> p a f", a=1).broadcast_to([P, AT, NE * NE])
            step(nc.vector.tensor_tensor(t3, t3, eb, ALU.mult))
            step(nc.vector.tensor_tensor(cmp, cmp, tie, ALU.add))
            step(nc.vector.tensor_reduce(rank, cmp.rearrange("p (t f) -> p t f", f=NE), AX_X, ALU.add))
            nc.vector.tensor_scalar(m0, rank, 0.0, None, ALU.is_equal)
            nc.vector.tensor_scalar(m1, rank, 1.0, None, ALU.is_equal)
            step(nc.vector.tensor_scalar(sel, rank, 1.5, None, ALU.is_lt))
            step(nc.vector.tensor_tensor(rank, m0, prob, ALU.mult))
            step(nc.vector.tensor_reduce(gates[:, 0, :], by_te(rank), AX_X, ALU.add))
            step(nc.vector.tensor_tensor(rank, m1, prob, ALU.mult))
            step(nc.vector.tensor_reduce(gates[:, 1, :], by_te(rank), AX_X, ALU.add))
            full(dve, mo_full, 0, 1)
            step(nc.vector.tensor_copy(tot.rearrange("p (e t) -> p e t", e=NE),
                                       mo[:, 1, AE:2 * AE].rearrange("p (t e) -> p e t", e=NE)))
            step(nc.vector.tensor_tensor_scan(incl, seg, tot, 0.0, ALU.mult, ALU.add))
            counts = incl.rearrange("p (e t) -> p e t", e=NE)[:, :, AT - 1:AT].broadcast_to([P, NE, 16])
            c3 = cnt.rearrange("p (e f) -> p e f", e=NE)
            step(nc.vector.tensor_tensor(c3, counts, steps.rearrange("p (a f) -> p a f", a=1).broadcast_to([P, NE, 16]),
                                         ALU.is_gt))
            step(nc.vector.tensor_reduce(ntile, c3, AX_X, ALU.add))
            step(nc.vector.tensor_tensor_scan(ends, ones[:, 0:NE], ntile, 0.0, ALU.mult, ALU.add))
            step(nc.vector.tensor_tensor(base_, ends, ntile, ALU.subtract))
            step(nc.vector.tensor_tensor(incl, incl, tot, ALU.subtract))
            i3 = incl.rearrange("p (e t) -> p e t", e=NE)
            step(nc.vector.scalar_tensor_tensor(
                out=i3, in0=base_.rearrange("p (e a) -> p e a", a=1).broadcast_to([P, NE, AT]), scalar=float(SLOTS),
                in1=i3, op0=ALU.mult, op1=ALU.add))
            step(nc.vector.tensor_tensor(by_te(slotf), by_te(mo[:, 1, 0:AE]), incl.rearrange("p (e t) -> p t e", e=NE),
                                         ALU.add))
            dve.sem_inc(mo_free[1], 1)
            step(nc.vector.tensor_tensor(m0, m0, slotf, ALU.mult))
            step(nc.vector.tensor_tensor(m1, m1, slotf, ALU.mult))
            step(nc.vector.tensor_reduce(red, by_te(m0), AX_X, ALU.add))
            step(nc.vector.tensor_copy(slots[:, 0, :], red))
            step(nc.vector.tensor_reduce(red, by_te(m1), AX_X, ALU.add))
            step(nc.vector.tensor_copy(slots[:, 1, :], red))
            step(nc.vector.tensor_tensor(ecmp.rearrange("p (t e) -> p t e", e=NE), over_e(ti, ZTILES),
                                         over_t(ends, ZTILES), ALU.is_ge))
            step(nc.vector.tensor_reduce(ef, ecmp.rearrange("p (t e) -> p t e", e=NE), AX_X, ALU.add))
            step(nc.vector.tensor_scalar(ef, ef, float(NE - 1), None, ALU.min))
            nc.vector.tensor_copy(eid[:, :], ef).then_inc(routed, 1)
            dve.wait_ge(routed, 1)
            dve.sem_inc(routed, 1)

            def do(kind, name, i, m, p):
                if kind == "S" and name == "SCAN":
                    s, c = i
                    if s == 0 and c == 0 and not (isinstance(m, int) and m == 0):
                        dve.wait_ge(carried, m * NS)
                        apart(dve)
                    dve.wait_ge(decay_ready, m * (NS * DC) + (s * DC + c + 1))
                    dve.wait_ge(dbu_ready, m * (NS * DC) + (s * DC + c + 1))
                    nc.vector.tensor_tensor_scan(h[:, s % 2, c, :], decay[:, c % 2, :], dbu[:, c % 2, :],
                                                 carry[:, p, s * DC + c:s * DC + c + 1], ALU.mult, ALU.add
                                                 ).then_inc(scanned, 1)
                elif kind == "S":
                    s = i[0]
                    dve.wait_ge(scanned, m * (NS * DC) + (s * DC + DC + 2))
                    nc.vector.tensor_copy(carry[:, p, s * DC:s * DC + DC], h[:, s % 2, :, BT - 1]).then_inc(carried, 1)
                elif kind == "Y":
                    s, j = i
                    dve.wait_ge(hT_ready, m * (NS * NT) + (s * NT + j + 1))
                    c_col = xdt[:, p, j, RK + NS + s:RK + NS + s + 1]
                    if s == 0:
                        if isinstance(m, int) and m == 0 and j == 0:
                            dve.wait_ge(scattered, 16 * 2 * AT)
                        nc.vector.tensor_scalar(acc[:, p, j, :], hT[:, j % 2, :], c_col, None, ALU.mult).then_inc(y_added, 1)
                    else:
                        nc.vector.scalar_tensor_tensor(out=acc[:, p, j, :], in0=hT[:, j % 2, :], scalar=c_col,
                                                       in1=acc[:, p, j, :], op0=ALU.mult, op1=ALU.add).then_inc(y_added, 1)
                elif kind == "A":
                    b = before_a(m)
                    if name == "XR":
                        dve.wait_ge(xa_in, m * 16 + 16)
                        for t in range(NT):
                            last = nc.vector.tensor_scalar(xa[:, t, :], xa[:, t, :], roots[:, 1, bass.ds(m * NT + t, 1)],
                                                           None, ALU.mult)
                        last.then_inc(xr_ready, 1)
                    elif name == "HALO":
                        if not isinstance(m, int) or m >= 2:
                            dve.wait_ge(halo_kept, m)
                        nc.vector.tensor_copy(xpad[:, :, 0:TAPS - 1], halo[:, p, :, :]).then_inc(halo_in, 1)
                    elif name[:2] == "CV":
                        c = int(name[2])
                        read_out(dve, ac_free, b, A_USES.index("IN%d" % c))
                        if c == 0:
                            dve.wait_ge(halo_in, m + 1)
                            dve.wait_ge(halved, 1)
                        w = [par[:, P_CONVW + c * TAPS + k:P_CONVW + c * TAPS + k + 1] for k in range(TAPS)]
                        nc.vector.tensor_scalar(xc[:, p, c, :], xpad[:, c, 0:BT], w[0], par[:, P_CONVB + c:P_CONVB + c + 1],
                                                ALU.mult, ALU.add).then_inc(conv, 1)
                        for k in range(1, TAPS):
                            dve.wait_ge(conv, m * (DC * TAPS) + (c * TAPS + k))
                            nc.vector.scalar_tensor_tensor(out=xc[:, p, c, :], in0=xpad[:, c, k:k + BT], scalar=w[k],
                                                           in1=xc[:, p, c, :], op0=ALU.mult, op1=ALU.add).then_inc(conv, 1)
                    elif name[:2] == "SL":
                        c = int(name[2])
                        dve.wait_ge(tanh_c, m * DC + (c + 1))
                        nc.vector.scalar_tensor_tensor(out=xc[:, p, c, :], in0=dtu[:, p, c, :], scalar=1.0,
                                                       in1=xc[:, p, c, :], op0=ALU.add, op1=ALU.mult).then_inc(xc_ready, 1)
                    elif name == "HKEEP":
                        nc.vector.tensor_copy(halo[:, p, :, :], xpad[:, :, BT:BT + TAPS - 1]).then_inc(halo_kept, 1)
                    elif name == "CT":
                        u = A_USES.index(name)
                        full(dve, ac_full, b, u)
                        nc.vector.tensor_copy(xdt[:, p, :, :].rearrange("p t d -> p (t d)"),
                                              ac[:, u % 2, 0:NT * XD]).then_inc(ac_free[u % 2], 1)
                    elif name == "DT":
                        dve.wait_ge(ln_done, m + 1)
                        nc.vector.tensor_tensor(dt[:, p, :, :], dt[:, p, :, :], dtu[:, p, :, :], ALU.add).then_inc(dt_ready, 1)
                    elif name == "DTU":
                        dve.wait_ge(dt_ready, m + 1)
                        nc.vector.tensor_tensor(dtu[:, p, :, :], dt[:, p, :, :], xc[:, p, :, :], ALU.mult).then_inc(dtu_ready, 1)
                elif kind == "C":
                    b = before_c(m)
                    if name[:2] == "YT":
                        c = int(name[2])
                        u = C_USES.index(name)
                        full(dve, ac_full, b, u)
                        nc.vector.scalar_tensor_tensor(out=xc[:, p, c, :], in0=xc[:, p, c, :],
                                                       scalar=par[:, P_D + c:P_D + c + 1], in1=ac[:, u % 2, :],
                                                       op0=ALU.mult, op1=ALU.add).then_inc(ac_free[u % 2], 1)
                    elif name[0] == "Z":
                        c = int(name[1])
                        u = C_USES.index(name)
                        dve.wait_ge(z_tanh, m * DC + (c + 1))
                        nc.vector.scalar_tensor_tensor(out=th[:, u % 2, :], in0=th[:, u % 2, :], scalar=1.0,
                                                       in1=ac[:, u % 2, :], op0=ALU.add, op1=ALU.mult).then_inc(z_silu, 1)
                        dve.wait_ge(z_silu, m * DC + (c + 1))
                        nc.vector.scalar_tensor_tensor(out=xc[:, p, c, :], in0=th[:, u % 2, :], scalar=0.5,
                                                       in1=xc[:, p, c, :], op0=ALU.mult, op1=ALU.mult
                                                       ).then_inc(ac_free[u % 2], 1)
                    elif name[:3] == "OUT":
                        u = C_USES.index(name)
                        t = 2 * int(name[3])
                        if t == 0:
                            dve.wait_ge(x1_in, m * 16 + 16)
                        full(dve, ac_full, b, u)
                        nc.vector.tensor_tensor(x1[:, t:t + 2, :], x1[:, t:t + 2, :],
                                                ac[:, u % 2, :].rearrange("p (t d) -> p t d", t=2), ALU.add
                                                ).then_inc(ac_free[u % 2], 1)
                    elif name == "RMS":
                        read_out(dve, ac_free, b, C_USES.index("OUT0"))
                        read_out(dve, ac_free, b, C_USES.index("OUT1"))
                        for t in range(NT):
                            last = nc.vector.bn_stats(cst[:, t, :], x1[:, t, :])
                        last.then_inc(rms, 1)
                        dve.wait_ge(rms, m * 6 + 1)
                        apart(dve)
                        for t in range(NT):
                            last = nc.vector.bn_aggr(cmv[:, t, :], cst[:, t, :])
                        last.then_inc(rms, 1)
                        dve.wait_ge(rms, m * 6 + 2)
                        nc.vector.tensor_tensor(cms[:, :], cmv[:, :, 0], cmv[:, :, 0], ALU.mult).then_inc(rms, 1)
                        dve.wait_ge(rms, m * 6 + 3)
                        nc.vector.tensor_tensor(cms[:, :], cms[:, :], cmv[:, :, 1], ALU.add).then_inc(rms, 1)
                        dve.wait_ge(rms, m * 6 + 4)
                        nc.vector.tensor_scalar(cms[:, :], cms[:, :], RMS_EPS, None, ALU.add).then_inc(rms, 1)
                        dve.wait_ge(rms, m * 6 + 5)
                        nc.vector.reciprocal(croot[:, :], cms[:, :]).then_inc(rms, 1)
                    elif name == "NORM":
                        dve.wait_ge(c_root, m + 1)
                        for t in range(NT):
                            last = nc.vector.tensor_scalar(xa[:, t, :], x1[:, t, :], croot[:, t:t + 1], None, ALU.mult)
                        last.then_inc(x1r_ready, 1)
                    elif name[:2] == "M1":
                        q, pair = int(name[2]), int(name[3])
                        u = C_USES.index(name)
                        dve.wait_ge(m_tanh, m * HC + (q * (HC // 2) + pair + 1))
                        nc.vector.scalar_tensor_tensor(
                            out=hid[:, 1, 2 * pair:2 * pair + 2, :].rearrange("p r t -> p (r t)"), in0=th[:, u % 2, :],
                            scalar=1.0, in1=ac[:, u % 2, :], op0=ALU.add, op1=ALU.mult).then_inc(ac_free[u % 2], 1)
                    elif name[:2] == "M2":
                        q, r = int(name[2]), int(name[3])
                        u = C_USES.index(name)
                        full(dve, ac_full, b, u)
                        nc.vector.scalar_tensor_tensor(out=x1[:, 2 * q + r, :], in0=ac[:, u % 2, 0:DM], scalar=0.5,
                                                       in1=x1[:, 2 * q + r, :], op0=ALU.mult, op1=ALU.add
                                                       ).then_inc(ac_free[u % 2], 1)

            walk(dve, do)
            for g in range(NB):
                b = g % 2
                dve.wait_ge(d_scaled, g + 1)
                for t in range(NT):
                    j = g * NT + t
                    last = nc.vector.scalar_tensor_tensor(out=gy[:, b, 0, t, :], in0=gy[:, b, 1, t, :],
                                                          scalar=gates[:, 1, j:j + 1], in1=gy[:, b, 0, t, :],
                                                          op0=ALU.mult, op1=ALU.add)
                last.then_inc(d_mixed, 1)
                if g >= 1:
                    finish(dve, g - 1)
            finish(dve, NB - 1)


def kernel(**inputs):
    import numpy as np
    import concourse.bacc as bacc
    from concourse.bass_utils import run_bass_kernel_spmd

    def a(name):
        return np.asarray(inputs[name])

    def rows(m):
        k = m.shape[0] // P
        return m.reshape(k, P, -1).transpose(1, 0, 2).reshape(P, -1)

    arrays = {
        "x": a("L0_attn_x").reshape(BATCH * SEQ, DM),
        "params": np.concatenate([
            rows(a("L0_attn_conv_w")), rows(a("L0_attn_conv_b").reshape(DI, 1)), rows(a("L0_attn_dt_proj_b").reshape(DI, 1)),
            rows(a("L0_attn_D").reshape(DI, 1)), a("L0_attn_A_log").reshape(DC, P, NS).transpose(1, 2, 0).reshape(P, -1),
            rows(a("L0_ffn_gate_w")), rows(a("L0_attn_x_proj_w").T)], axis=1),
        "weights": np.concatenate([rows(a("L0_attn_in_proj_w").T), rows(a("L0_attn_out_proj_w").T)], axis=1),
        "w_dt": a("L0_attn_dt_proj_w").T,
        "moe1": np.stack([np.concatenate([rows(a("L0_ffn_w1")[e]), rows(a("L0_ffn_b1")[e].reshape(HID, 1))], axis=1)
                          for e in range(NE)]),
        "moe2": np.stack([rows(a("L0_ffn_w2")[e]) for e in range(NE)]),
        "moe_b2": a("L0_ffn_b2"),
        "gate_b": a("L0_ffn_gate_b"),
        "mlp": np.concatenate([rows(a("L0_attn_mlp_w1").T), rows(a("L0_attn_mlp_w2").T)], axis=1),
    }
    arrays = {k: np.ascontiguousarray(v) for k, v in arrays.items()}
    nc = bacc.Bacc("TRN2", target_bir_lowering=False, num_devices=1)
    args = [nc.dram_tensor(k, v.shape, F32, kind="ExternalInput").ap() for k, v in arrays.items()]
    out = nc.dram_tensor("out", (BATCH * SEQ, DM), F32, kind="ExternalOutput").ap()

    def scratch(name, shape):
        return nc.dram_tensor(name, shape, F32, kind="Internal").ap()

    mamba_moe(nc, *args, out, scratch("b_rows", (NB * NS, BT)), scratch("xn_rows", (BATCH * SEQ, DM)),
              scratch("s_rows", (BATCH * SEQ, DM)), scratch("slot_x", (ZTILES * SLOTS, DM)),
              scratch("slot_y", (TILES * SLOTS, DM)))
    r = run_bass_kernel_spmd(nc, [arrays], core_ids=[0])
    return r.results[0]["out"].reshape(BATCH, SEQ, DM)
```

```python
from contextlib import ExitStack

import concourse.bass as bass
from concourse import mybir

F32 = mybir.dt.float32
I32 = mybir.dt.int32
ALU = mybir.AluOpType
ACT = mybir.ActivationFunctionType
AX_X = mybir.AxisListType.X

P = 128
BATCH, SEQ, DM = 2, 2048, 256
DI = 2 * DM
NS = 16
RK = 16
XD = RK + 2 * NS
TAPS = 4
NE, HID = 8, 1024
BT = 512
NB = BATCH * SEQ // BT
NT = BT // P
AT = NB * NT
KC = DM // P
DC = DI // P
HC = HID // P
SLOTS = 256
TILES = (2 * BATCH * SEQ + NE * (SLOTS - 1)) // SLOTS
ZTILES = TILES + 1
LN_EPS = 1e-5
RMS_EPS = 1.1920929e-07

P_CONVW = 0
P_CONVB = P_CONVW + DC * TAPS
P_DTB = P_CONVB + DC
P_D = P_DTB + DC
P_ALOG = P_D + DC
P_GATE = P_ALOG + NS * DC
P_XPROJ = P_GATE + KC * NE
P_END = P_XPROJ + DC * XD
W1_COLS = KC * HID + HC

A_USES = ["TR0", "TR1", "IN0", "IN1", "IN2", "IN3", "XD0", "XD1", "DT0", "DT1", "DT2", "DT3"]
C_USES = (["Z%d" % c for c in range(DC)] + ["OUT0", "OUT1", "T10", "T11"]
          + [w % q for q in range(2) for w in ("M1%d0", "M1%d1", "M1%d2", "M1%d3", "M2%d0", "M2%d1")])
M_USES = ["UP0", "UP1", "UP2", "UP3", "MT", "DN0", "DN1"]
PRE_C = NB * KC
PRE_M = 4
PER_BODY = 6
FIRST_BODY = 1
assert PER_BODY * (NB - 1 - FIRST_BODY) < TILES <= PER_BODY * (NB - FIRST_BODY)
assert PRE_C % 2 == 0 and len(A_USES) % 2 == 0 and len(C_USES) % 2 == 0 and PER_BODY * len(M_USES) % 2 == 0

A_WORK = {"LOADX": 0, "XR": 8, "TR0": 12, "TR1": 13, "HALO": 14, "IN0": 15, "IN1": 17, "IN2": 19, "IN3": 21,
          "CV0": 24, "SL0": 28, "CV1": 29, "SL1": 33, "CV2": 34, "SL2": 38, "CV3": 39, "SL3": 43, "HKEEP": 43,
          "XD0": 45, "XD1": 47, "BOUT": 48, "DT0": 50, "DT1": 51, "DT2": 52, "DT3": 53, "SP": 54, "DT": 57, "DTU": 59}
C_WORK = (["LOADN"] + ["Z%d" % c for c in range(DC)]
          + ["OUT0", "OUT1", "RMS", "NORM", "T10", "T11"]
          + [w % q for q in range(2) for w in ("M1%d0", "M1%d1", "M1%d2", "M1%d3", "M2%d0", "M2%d1")] + ["STORE"])
R_STEP = 2
R_AT = 18
L_AFTER = {"XR": ("L1", "L2"), "IN3": ("L3",), "CV0": ("L4",), "CV1": ("L5",), "CV2": ("L6",), "CV3": ("L7",),
           "HKEEP": ("ROOT",), "DT3": ("XN",)}
R_SLOTS = {}
for g in range(NB):
    R_SLOTS.setdefault(1 + R_STEP * g, []).extend(["TX%d0" % g, "TX%d1" % g])
    R_SLOTS.setdefault(1 + R_STEP * g + R_STEP, []).append("LG%d" % g)
for i in range(8):
    R_SLOTS.setdefault(R_AT + i + (i > 3), []).append("RO%d" % i)
R_SLOTS.setdefault(R_AT + 4, []).append("BL")
for t in range(AT):
    R_SLOTS.setdefault(R_AT + 9 + t * (NS * DC - 10 - R_AT) // AT, []).append("SC%d" % t)
D_AFTER = {4 + 3 * g: (g,) for g in range(NB - 1)}
M_WORK = ["UP0", "UP1", "UP2", "UP3", "MT", "DN0", "DN1", "NEXT"]


COST = {"UP": 4, "MT": 1, "DN": 8, "TR": 1, "IN": 4, "XD": 4, "DT": 2, "Z": 4, "OU": 8, "T1": 1,
        "M1": 4, "M2": 8}


def cost(name):
    if name in ("DT", "DTU"):
        return 0
    return COST.get(name[:2], COST.get(name[:1], 0))


DELAY = {"LOADN": 0, "RMS": 12, "NORM": 12, "T11": 4, "OUT1": 4, "Z3": 4}


def spread(work, first, last):
    weight = [cost(w) + DELAY.get(w, 0) + C_WAIT for w in work]
    return {i: [w for k, w in enumerate(work) if first + sum(weight[:k]) * (last - first) // sum(weight) == i]
            for i in range(first, last)}


def fill(work, n, others, limit):
    work = list(work)
    total = sum(cost(w) for w, t in work) + sum(others)
    slots, done = {}, 0
    for i in range(n):
        done += others[i]
        slots[i] = []
        while work and (i == n - 1 or (done + cost(work[0][0]) / 2 < total * (i + 1) / n
                                       and sum(cost(w) > 0 for w, t in slots[i]) < limit)):
            done += cost(work[0][0])
            slots[i].append(work.pop(0))
    return slots


C_START, C_END, C_WAIT = 4, 56, 1
LIMIT = 2
OWN_DBU = (3,)
OWN_HC = (3,)
LATER = {"act": {"R": 1, "M": 1, "C": 1, "A": 1}, "dve": {"Y": 3, "M": 1, "C": 1, "A": 0}, "pool": {"Y": 2}}


def schedule(with_c, with_a, tiles, later, router):
    n = NS * DC
    work = {"C": spread(C_WORK, C_START, C_END) if with_c else {},
            "A": {i: [w for w in A_WORK if A_WORK[w] == i] for i in range(n)} if with_a else {}}
    work["M"] = fill([(w, t) for t in range(tiles) for w in M_WORK], n,
                     [sum(cost(w) for k in "CA" for w in work[k].get(i, [])) for i in range(n)], LIMIT)
    order = []
    for i in range(n + 2):
        if i < n:
            order.append(("S", "SCAN", (i // DC, i % DC)))
        for kind in ("R", "Y", "M", "C", "A"):
            j = i - later.get(kind, 0)
            if kind == "R" and router:
                order += [("R", w, None) for w in R_SLOTS.get(j, [])]
            if kind == "Y" and i < n:
                order.append(("Y", "ADD", (j // DC, j % DC)))
            elif kind == "M":
                order += [("M", w, t) for w, t in work["M"].get(j, [])]
            elif kind in ("C", "A"):
                order += [(kind, w, None) for w in work[kind].get(j, [])]
        if i % DC == DC - 1 and i < n:
            order.append(("S", "KEEP", (i // DC, None)))
    return order


def mamba_moe(nc, x, params, weights, w_dt, moe1, moe2, moe_b2, gate_b, mlp, out, bc_rows, xn_rows, s_rows,
              slot_x, slot_y):
    with ExitStack() as ctx:
        def sb(name, shape, dtype=F32):
            return ctx.enter_context(nc.sbuf_tensor(name, shape, dtype))

        def sem(name):
            return ctx.enter_context(nc.semaphore(name))

        par = sb("par", [P, P_END])
        wts = sb("wts", [P, KC * 2 * DI + DC * DM])
        w_in = wts[:, 0:KC * 2 * DI].rearrange("p (k n) -> p k n", k=KC)
        w_out = wts[:, KC * 2 * DI:].rearrange("p (k n) -> p k n", k=DC)
        wdt = sb("wdt", [RK, DI])
        wm = sb("wm", [P, KC * HID + HC * DM])
        wm1 = wm[:, 0:KC * HID].rearrange("p (k n) -> p k n", k=KC)
        wm2 = wm[:, KC * HID:].rearrange("p (k n) -> p k n", k=HC)
        ident = sb("ident", [P, P])
        ones = sb("ones", [P, P])
        below = sb("below", [P, P])
        late = sb("late", [P, 2 * HC * SLOTS + W1_COLS + HC * DM])
        hid = late[:, 0:2 * HC * SLOTS].rearrange("p (b k t) -> p b k t", b=2, k=HC)
        w1 = late[:, 2 * HC * SLOTS:2 * HC * SLOTS + W1_COLS]
        w2 = late[:, 2 * HC * SLOTS + W1_COLS:].rearrange("p (k n) -> p k n", k=HC)
        xn_all = late[:, 0:AT * DM].rearrange("p (t d) -> p t d", t=AT)
        w1v = w1[:, 0:KC * HID].rearrange("p (k n) -> p k n", k=KC)
        b2row = sb("b2row", [1, DM])
        xs = sb("xs", [P, 2, 2, DM])
        xsT = sb("xsT", [P, KC, SLOTS])
        ys = sb("ys", [P, 2, 2, DM])
        xa = sb("xa", [P, NT, DM])
        x1 = sb("x1", [P, NT, DM])
        xrT = sb("xrT", [P, 2, KC, BT])
        xpad = sb("xpad", [P, DC, TAPS - 1 + BT])
        xb = sb("xb", [P, NT, DM])
        xc = sb("xc", [P, 2, DC, BT])
        dt = sb("dt", [P, 2, DC, BT])
        dtu = sb("dtu", [P, 2, DC, BT])
        xdT = sb("xdT", [XD, BT])
        th = sb("th", [P, 2, BT])
        halo = sb("halo", [P, 2, DC, TAPS - 1])
        carry = sb("carry", [P, 2, NS * DC])
        h = sb("h", [P, 2, DC, BT])
        bb = sb("bb", [P, 2, BT])
        cb = sb("cb", [P, 2, BT])
        dbu = sb("dbu", [P, DC, BT])
        hxc = sb("hxc", [P, 2, BT])
        st = sb("st", [P, AT, 6])
        cst = sb("cst", [P, NT, 6])
        mv = sb("mv", [P, AT, 2])
        roots = sb("roots", [P, 2, AT])
        ms = sb("ms", [P, AT])
        cmv = sb("cmv", [P, NT, 2])
        cms = sb("cms", [P, NT])
        croot = sb("croot", [P, NT])
        slots = sb("slots", [P, 2, AT], I32)
        gates = sb("gates", [P, 2, AT])
        eid = sb("eid", [P, ZTILES], I32)
        cmp, tie = wm[:, 0:AT * NE * NE], wm[:, AT * NE * NE:2 * AT * NE * NE]
        xs_flat = xs[:, :, :, :].rearrange("p b r d -> p (b r d)")
        ys_flat = ys[:, :, :, :].rearrange("p b r d -> p (b r d)")
        xsT_flat = xsT[:, :, :].rearrange("p k t -> p (k t)")
        xnT = (th, ys_flat.rearrange("p (k t) -> p k t", k=KC))
        AE = AT * NE
        lg, prob, rank, sel = (xs_flat[:, i * AE:(i + 1) * AE] for i in range(4))
        m0, m1, tot, incl = (ys_flat[:, i * AE:(i + 1) * AE] for i in range(4))
        slotf, seg = (xsT_flat[:, i * AE:(i + 1) * AE] for i in range(2))
        x1_flat = x1[:, :, :].rearrange("p t d -> p (t d)")
        EARLY, GATEB, RED, CNT, COUNTS, NTILE, ENDS, BASE, STEPS, TI, EF = 0, 64, 72, 104, 112, 240, 248, 256, 264, 280, 328
        earlier = x1_flat[:, EARLY:EARLY + NE * NE]
        gateb = x1_flat[:, GATEB:GATEB + NE]
        red = x1_flat[:, RED:RED + AT]
        cnt = x1_flat[:, COUNTS:COUNTS + NE * 16]
        ntile = x1_flat[:, NTILE:NTILE + NE]
        ends = x1_flat[:, ENDS:ENDS + NE]
        base_ = x1_flat[:, BASE:BASE + NE]
        steps = x1_flat[:, STEPS:STEPS + 16]
        ti = x1_flat[:, TI:TI + ZTILES]
        ef = x1_flat[:, EF:EF + ZTILES]
        ecmp = x1_flat[:, 384:384 + ZTILES * NE]
        zeros = xb[:, :, :].rearrange("p t d -> p (t d)")
        ZROWS = NT * P
        gy = dt[:, :, :, :].rearrange("p b c t -> p (b c t)").rearrange("p (b k t d) -> p b k t d", b=2, k=2, t=NT)
        sx = dtu[:, :, :, :].rearrange("p b c t -> p (b c t)").rearrange("p (b k t d) -> p b k t d", b=2, k=2, t=NT)

        decay = ctx.enter_context(nc.psum_tensor("decay", [P, 2, BT], F32))
        aa = ctx.enter_context(nc.psum_tensor("aa", [P, 2, 512], F32))
        ac = ctx.enter_context(nc.psum_tensor("ac", [P, 2, 512], F32))
        mo = ctx.enter_context(nc.psum_tensor("mo", [P, 2, 512], F32))

        params_in = sem("params_in")
        wm_in = sem("wm_in")
        consts = sem("consts")
        aside = sem("aside")
        aa_full = [sem("aa_full0"), sem("aa_full1")]
        aa_free = [sem("aa_free0"), sem("aa_free1")]
        ac_full = [sem("ac_full0"), sem("ac_full1")]
        ac_free = [sem("ac_free0"), sem("ac_free1")]
        mo_full = [sem("mo_full0"), sem("mo_full1")]
        mo_free = [sem("mo_free0"), sem("mo_free1")]
        x_in = [sem("x_in%d" % g) for g in range(NB)]
        neg_a_ready = sem("neg_a_ready")
        halved = sem("halved")
        stats = sem("stats")
        ln_root = sem("ln_root")
        xn_ready = sem("xn_ready")
        xn_out = sem("xn_out")
        zero_out = sem("zero_out")
        router = sem("router")
        router_exp = sem("router_exp")
        routed = sem("routed")
        scattered = sem("scattered")
        xa_in = sem("xa_in")
        xr_ready = sem("xr_ready")
        halo_in = sem("halo_in")
        conv = sem("conv")
        tanh_c = sem("tanh_c")
        xc_ready = sem("xc_ready")
        halo_kept = sem("halo_kept")
        b_out = sem("b_out")
        softplus = sem("softplus")
        ln_done = sem("ln_done")
        dt_ready = sem("dt_ready")
        dtu_ready = sem("dtu_ready")
        bb_in = [sem("bb_in0"), sem("bb_in1")]
        decay_ready = sem("decay_ready")
        dbu_ready = sem("dbu_ready")
        own_dbu_ready = sem("own_dbu_ready")
        cb_in = [sem("cb_in0"), sem("cb_in1")]
        hc_ready = sem("hc_ready")
        own_hc_ready = sem("own_hc_ready")
        scanned = sem("scanned")
        carried = sem("carried")
        y_added = sem("y_added")
        x1_in = sem("x1_in")
        z_tanh = sem("z_tanh")
        z_silu = sem("z_silu")
        rms = sem("rms")
        c_root = sem("c_root")
        x1r_ready = sem("x1r_ready")
        m_tanh = sem("m_tanh")
        s_out = sem("s_out")
        w1_in = sem("w1_in")
        w2_in = sem("w2_in")
        xs_in = [sem("xs_in0"), sem("xs_in1")]
        ys_out = [sem("ys_out0"), sem("ys_out1")]
        gathered = [sem("gathered0"), sem("gathered1")]
        sx_in = [sem("sx_in0"), sem("sx_in1")]
        d_scaled = sem("d_scaled")
        d_mixed = sem("d_mixed")
        d_gate = sem("d_gate")
        d_prod = sem("d_prod")
        d_ready = sem("d_ready")
        stored = [sem("stored0"), sem("stored1")]

        x_t = x.rearrange("(b h t p) d -> h b p t d", b=BATCH, t=NT, p=P)
        out_t = out.rearrange("(b h t p) d -> h b p t d", b=BATCH, t=NT, p=P)
        xn_t = xn_rows.rearrange("(m p t) d -> m p (t d)", p=P, t=NT)
        s_t = s_rows.rearrange("(m p t) d -> m p (t d)", p=P, t=NT)
        slot_x_t = slot_x.rearrange("(i p r) d -> i p (r d)", p=P, r=2)
        slot_y_t = slot_y.rearrange("(i p r) d -> i p (r d)", p=P, r=2)

        def x1T(m, p):
            if isinstance(m, int) and m == NB - 1:
                return xpad[:, 0:KC, 0:BT]
            return dt[:, p, 0:KC, :]

        def flat3(ap):
            return ap.rearrange("p t d -> p (t d)")

        def before_a(m):
            return m * (len(A_USES) // 2)

        def before_c(m):
            return m * (len(C_USES) // 2) + PRE_C // 2

        def before_m(n):
            return (n - FIRST_BODY) * (PER_BODY * len(M_USES) // 2) + PRE_M // 2

        def wait_formed(eng, own, sems, m, s, chunks):
            for sem_, made in ((sems[0], [c for c in range(DC) if c not in own]), (sems[1], list(own))):
                wanted = [i for i, c in enumerate(made) if c in chunks]
                if wanted:
                    if len(chunks) > 1 and sem_ is sems[1]:
                        apart(eng)
                    eng.wait_ge(sem_, m * (NS * len(made)) + (s * len(made) + wanted[-1] + 1))

        def wait_dbu(eng, m, s, chunks):
            wait_formed(eng, OWN_DBU, (dbu_ready, own_dbu_ready), m, s, chunks)

        def wait_hc(eng, m, s, chunks):
            wait_formed(eng, OWN_HC, (hc_ready, own_hc_ready), m, s, chunks)

        def full(eng, sems, before, u):
            eng.wait_ge(sems[u % 2], before + (u // 2 + 1))

        def free(eng, sems, before, u):
            eng.wait_ge(sems[u % 2], before + (u // 2 + 1))

        def read_out(eng, sems, before, u):
            eng.wait_ge(sems[u % 2], before + (u // 2 + 2))

        def apart(eng):
            eng.sem_inc(aside, 1)

        def walk(eng, do, later={}):
            def body(n, p, with_c, with_a, tiles, router=False):
                for kind, name, i in schedule(with_c, with_a, tiles, later, router):
                    if kind == "S":
                        do(kind, name, i, n, p)
                    elif kind == "Y" and i[0] >= 0:
                        do(kind, name, i, n, p)
                    elif kind == "Y" and with_c:
                        do(kind, name, (NS + i[0], i[1]), n - 1, 1 - p)
                    elif kind == "C":
                        do(kind, name, i, n - 1, 1 - p)
                    elif kind == "A":
                        do(kind, name, i, n + 1, 1 - p)
                    elif kind in ("M", "R"):
                        do(kind, name, i, n, p)

            for name in A_WORK:
                do("A", name, None, 0, 0)
                for norm in L_AFTER.get(name, ()):
                    do("L", norm, None, None, None)
            body(0, 0, False, True, 0, True)
            do("M", "START", None, 0, 0)
            with eng.Fori(0, (NB - 2) // 2) as i:
                body(i * 2 + 1, 1, True, True, PER_BODY)
                body(i * 2 + 2, 0, True, True, PER_BODY)
            body(NB - 1, 1, True, False, TILES - PER_BODY * (NB - 1 - FIRST_BODY))
            for k in range(NS * DC - later.get("Y", 0), NS * DC):
                do("Y", "ADD", (k // DC, k % DC), NB - 1, 1)
            for k, name in enumerate(C_WORK):
                do("C", name, None, NB - 1, 1)
                for g in D_AFTER.get(k, ()):
                    do("D", None, g, None, None)
            do("D", None, NB - 1, None, None)

        CONSTS = 14
        NORM_STEPS = 7
        AE = AT * NE
        neg_a = par[:, P_ALOG:P_ALOG + NS * DC]

        def x_dst(g):
            return xn_all[:, g * NT:(g + 1) * NT, :]

        def is_last_tile(m, i):
            return int(isinstance(m, int) and (m - FIRST_BODY) * PER_BODY + i == TILES - 1)

        def store(sp, g):
            sp.wait_ge(d_ready, g + 1)
            sp.dma_start(out_t[g // 2, g % 2], sx[:, g % 2, 0]).then_inc(stored[g % 2], 16)

        def finish(dve, g):
            b = g % 2
            dve.wait_ge(d_gate, g + 1)
            dve.wait_ge(sx_in[b], 32 * (g // 2 + 1))
            nc.vector.tensor_tensor(sx[:, b, 0], sx[:, b, 0], gy[:, b, 0], ALU.mult).then_inc(d_prod, 1)
            dve.wait_ge(d_prod, g + 1)
            nc.vector.tensor_tensor(sx[:, b, 0], sx[:, b, 0], sx[:, b, 1], ALU.add).then_inc(d_ready, 1)

        block = ctx.enter_context(nc.Block())

        @block.sync
        def _(sp):
            sp.dma_start(x_dst(0), x_t[0, 0]).then_inc(x_in[0], 16)
            sp.dma_start(par[:, :], params).then_inc(params_in, 16)
            sp.dma_start(wts[:, :], weights).then_inc(params_in, 16)
            sp.dma_start(wdt[:, :], w_dt).then_inc(params_in, 16)
            sp.dma_start(gateb, gate_b.partition_broadcast(P)).then_inc(params_in, 16)
            for g in range(1, NB):
                sp.dma_start(x_dst(g), x_t[g // 2, g % 2]).then_inc(x_in[g], 16)

            def load_first(i):
                apart(sp)
                e = sp.value_load(eid[0:1, bass.ds(i, 1)], min_val=0, max_val=NE - 1)
                sp.dma_start(w1[:, :], moe1[bass.ds(e, 1)].rearrange("a p n -> p (a n)")).then_inc(w1_in, 16)

            def load_second(i):
                apart(sp)
                e = sp.value_load(eid[0:1, bass.ds(i, 1)], min_val=0, max_val=NE - 1)
                sp.dma_start(w2[:, :, :].rearrange("p k n -> p (k n)"),
                             moe2[bass.ds(e, 1)].rearrange("a p n -> p (a n)")).then_inc(w2_in, 16)
                sp.dma_start(b2row[:, :], moe_b2[bass.ds(e, 1)]).then_inc(w2_in, 16)

            def load_rows(i, slot):
                sp.dma_start(xs[:, slot, :, :].rearrange("p r d -> p (r d)"),
                             slot_x_t[bass.ds(i, 1)].rearrange("a p n -> p (a n)")).then_inc(xs_in[slot], 16)

            def load_b(m, s):
                sp.dma_start(bb[:, s % 2, :], bc_rows[bass.ds(m * (2 * NS) + s, 1), :].rearrange("a t -> (a t)")
                             .partition_broadcast(P)).then_inc(bb_in[s % 2], 16)

            def load_c(m, s):
                if s >= 2 or not (isinstance(m, int) and m == 0):
                    wait_hc(sp, m, s - 2, range(DC))
                    apart(sp)
                sp.dma_start(cb[:, s % 2, :], bc_rows[bass.ds(m * (2 * NS) + (NS + s), 1), :].rearrange("a t -> (a t)")
                             .partition_broadcast(P)).then_inc(cb_in[s % 2], 16)

            def do(kind, name, i, m, p):
                if kind == "S" and name == "SCAN" and i[1] == DC - 1 and i[0] < NS - 1:
                    load_c(m, i[0] + 1)
                elif kind == "S" and name == "SCAN" and i[1] == 0:
                    s = i[0]
                    if s == 0:
                        sp.wait_ge(b_out, m * 16 + 16)
                        apart(sp)
                        if not (isinstance(m, int) and m == 0):
                            wait_dbu(sp, m, -1, range(DC))
                            apart(sp)
                        load_b(m, 0)
                        load_b(m, 1)
                        load_c(m, 0)
                    elif s < NS - 1:
                        wait_dbu(sp, m, s - 1, range(DC))
                        apart(sp)
                        load_b(m, s + 1)
                elif kind == "L" and name == "XN":
                    for g in range(NB):
                        sp.wait_ge(xn_ready, g * NT + NT)
                        sp.dma_start(xn_t[g], flat3(xn_all[:, g * NT:(g + 1) * NT, :])).then_inc(xn_out, 16)
                elif kind == "R" and name == "RO7":
                    sp.wait_ge(routed, 2)
                    sp.dma_start(wm[:, :], mlp).then_inc(wm_in, 16)
                elif kind == "A" and name == "LOADX":
                    if isinstance(m, int) and m == 0:
                        return
                    if isinstance(m, int) and m == 1:
                        sp.wait_ge(xn_out, 16 * NB)
                    if not (isinstance(m, int) and m == 0):
                        full(sp, aa_full, before_a(m - 1), A_USES.index("TR1"))
                    sp.dma_start(flat3(xa[:, :, :]), xn_t[bass.ds(m, 1)].rearrange("a p n -> p (a n)")).then_inc(xa_in, 16)
                elif kind == "C" and name == "LOADN":
                    sp.wait_ge(s_out, m * 16 + 16)
                    if isinstance(m, int) is False or m == 0:
                        sp.wait_ge(routed, 2)
                    sp.dma_start(flat3(x1[:, :, :]), xn_t[bass.ds(m, 1)].rearrange("a p n -> p (a n)")).then_inc(x1_in, 16)
                elif kind == "C" and name == "STORE":
                    read_out(sp, ac_free, before_c(m), C_USES.index("M210"))
                    read_out(sp, ac_free, before_c(m), C_USES.index("M211"))
                    sp.dma_start(s_t[bass.ds(m, 1)].rearrange("a p n -> p (a n)"), flat3(x1[:, :, :])).then_inc(s_out, 16)
                elif kind == "D":
                    g = i
                    if g == 0:
                        sp.wait_ge(scanned, NB * NS * DC + DC)
                        sp.wait_ge(s_out, 16 + 16 * (NB - 1))
                    if g == NB - 1:
                        sp.wait_ge(s_out, 16 + 16 * NB)
                    if g >= 2:
                        sp.wait_ge(stored[g % 2], 16 * (g // 2))
                    sp.dma_start(flat3(sx[:, g % 2, 0]), s_t[g]).then_inc(sx_in[g % 2], 16)
                    sp.dma_start(sx[:, g % 2, 1], x_t[g // 2, g % 2]).then_inc(sx_in[g % 2], 16)
                    if g >= 1:
                        store(sp, g - 1)
                elif kind == "M":
                    if name == "START":
                        sp.wait_ge(scattered, 16 * 2 * AT)
                        load_first(0)
                        load_rows(0, 0)
                        load_second(0)
                        load_rows(1, 1)
                        return
                    tile = (m - FIRST_BODY) * PER_BODY + i
                    last = isinstance(m, int) and tile == TILES - 1
                    if name == "MT" and not last:
                        read_out(sp, mo_free, before_m(m), i * len(M_USES) + M_USES.index("UP3"))
                        load_first(tile + 1)
                    elif name == "NEXT" and not last:
                        full(sp, mo_full, before_m(m), i * len(M_USES) + M_USES.index("DN1"))
                        load_second(tile + 1)
                        if not (isinstance(m, int) and tile == TILES - 2):
                            load_rows(tile + 2, i % 2)

            walk(sp, do)
            store(sp, NB - 1)
            for b in range(2):
                sp.wait_ge(stored[b], 16 * NB // 2)
                sp.wait_ge(ys_out[b], 16 * ((TILES + 1 - b) // 2) + 16)

        @block.gpsimd
        def _(pool):
            def iota(dst, pattern, cm=0):
                nc.gpsimd.iota(dst, pattern, base=0, channel_multiplier=cm,
                               allow_small_or_imprecise_dtypes=True).then_inc(consts, 1)
            nc.gpsimd.memset(ident[:, :], 0.0).then_inc(consts, 1)
            nc.gpsimd.memset(below[:, :], 0.0).then_inc(consts, 1)
            nc.gpsimd.memset(earlier, 0.0).then_inc(consts, 1)
            nc.gpsimd.memset(seg, 1.0).then_inc(consts, 1)
            pool.wait_ge(consts, 4)
            nc.gpsimd.affine_select(out=ident[:, :], in_=ident[:, :], compare_op=ALU.not_equal, fill=1.0,
                                    base=0, pattern=[[-1, P]], channel_multiplier=1).then_inc(consts, 1)
            nc.gpsimd.affine_select(out=below[:, :], in_=below[:, :], compare_op=ALU.is_ge, fill=1.0,
                                    base=0, pattern=[[-1, P]], channel_multiplier=1).then_inc(consts, 1)
            e3 = earlier.rearrange("p (e f) -> p e f", e=NE)
            nc.gpsimd.affine_select(out=e3, in_=e3, compare_op=ALU.is_ge, fill=1.0,
                                    base=0, pattern=[[-1, NE], [1, NE]], channel_multiplier=0).then_inc(consts, 1)
            nc.gpsimd.memset(seg.rearrange("p (e t) -> p e t", e=NE)[:, :, 0:1], 0.0).then_inc(consts, 1)
            nc.gpsimd.memset(ones[:, :], 1.0).then_inc(consts, 1)
            nc.gpsimd.memset(zeros, 0.0).then_inc(consts, 1)
            iota(steps, [[SLOTS, 16]])
            iota(ti, [[1, ZTILES]])
            nc.gpsimd.memset(halo[:, :, :, :], 0.0).then_inc(consts, 1)
            nc.gpsimd.memset(carry[:, :, :], 0.0).then_inc(consts, 1)

            pool.wait_ge(consts, CONSTS)
            for i in range(ZTILES * SLOTS // ZROWS):
                pool.dma_start(slot_x[i * ZROWS:(i + 1) * ZROWS, :].rearrange("(p t) d -> p (t d)", p=P),
                               zeros).then_inc(zero_out, 16)

            def scatter(j):
                for k in range(2):
                    pool.indirect_dma_start(
                        out=slot_x, out_offset=bass.IndirectOffsetOnAxis(ap=slots[:, k, j:j + 1], axis=0),
                        in_=xn_all[:, j, :], in_offset=None).then_inc(scattered, 16)

            def do(kind, name, i, m, p):
                if kind == "S" and name == "SCAN":
                    s, c = i
                    if s == 0 and c == 0:
                        pool.wait_ge(dtu_ready, m + 1)
                    if c == 0:
                        pool.wait_ge(bb_in[s % 2], m * (NS * 8) + (s // 2 * 16 + 16))
                    if c in OWN_DBU:
                        return
                    pool.wait_ge(scanned, m * (NS * DC) + (s * DC + c + 1))
                    nc.gpsimd.tensor_tensor(dbu[:, c, :], dtu[:, p, c, :], bb[:, s % 2, :],
                                            ALU.mult).then_inc(dbu_ready, 1)

                elif kind == "Y":
                    s, c = i
                    if c == 0:
                        pool.wait_ge(cb_in[s % 2], m * (NS * 8) + (s // 2 * 16 + 16))
                        apart(pool)
                    if c in OWN_HC:
                        return
                    pool.wait_ge(scanned, m * (NS * DC) + (s * DC + c + 1 + DC))
                    pool.wait_ge(y_added, m * (NS * DC) + (s * DC + c + 1))
                    nc.gpsimd.tensor_tensor(hxc[:, c % 2, :], h[:, s % 2, c, :], cb[:, s % 2, :],
                                            ALU.mult).then_inc(hc_ready, 1)
                elif kind == "R" and name[:2] == "SC":
                    if name == "SC0":
                        pool.wait_ge(routed, 2)
                        pool.wait_ge(zero_out, 16 * (ZTILES * SLOTS // ZROWS))
                    scatter(int(name[2:]))
                elif kind == "D":
                    g = i
                    if g == 0:
                        pool.wait_ge(scanned, NB * NS * DC + DC)
                        for b in range(2):
                            pool.wait_ge(ys_out[b], 16 * ((TILES + 1 - b) // 2) + 16)
                    if g >= 2:
                        pool.wait_ge(d_prod, g - 1)
                    for t in range(NT):
                        for k in range(2):
                            pool.indirect_dma_start(
                                out=gy[:, g % 2, k, t, :], out_offset=None, in_=slot_y,
                                in_offset=bass.IndirectOffsetOnAxis(ap=slots[:, k, g * NT + t:g * NT + t + 1], axis=0)
                            ).then_inc(gathered[g % 2], 16)

            walk(pool, do, LATER["pool"])

        @block.scalar
        def _(act):
            act.wait_ge(stats, NORM_STEPS)
            nc.scalar.activation(roots[:, :, 0:NT], roots[:, :, 0:NT], ACT.Sqrt).then_inc(ln_root, 1)
            act.wait_ge(params_in, 64)
            nc.scalar.activation(neg_a, neg_a, ACT.Exp).then_inc(neg_a_ready, 1)
            act.wait_ge(neg_a_ready, 1)
            nc.scalar.mul(neg_a, neg_a, -1.0).then_inc(neg_a_ready, 1)

            def do(kind, name, i, m, p):
                if kind == "S" and name == "SCAN":
                    s, c = i
                    if s == 0 and c == 0:
                        act.wait_ge(dt_ready, m + 1)
                        act.wait_ge(neg_a_ready, 2)
                    act.wait_ge(scanned, m * (NS * DC) + (s * DC + c + 1 + 2))
                    nc.scalar.activation(decay[:, c % 2, :], dt[:, p, c, :], ACT.Exp,
                                         scale=par[:, P_ALOG + s * DC + c:P_ALOG + s * DC + c + 1]).then_inc(decay_ready, 1)
                elif kind == "A":
                    b = before_a(m)
                    if name[:2] == "TR":
                        k = int(name[2])
                        u = A_USES.index(name)
                        if k == 0 and not (isinstance(m, int) and m < 2):
                            full(act, ac_full, before_c(m - 2), C_USES.index("Z3"))
                        full(act, aa_full, b, u)
                        nc.scalar.copy(xrT[:, p, k, :], aa[:, u % 2, :]).then_inc(aa_free[u % 2], 1)
                    elif name[:2] == "IN":
                        c = int(name[2])
                        u = A_USES.index(name)
                        full(act, aa_full, b, u)
                        nc.scalar.copy(xpad[:, c, TAPS - 1:], aa[:, u % 2, :]).then_inc(aa_free[u % 2], 1)
                    elif name[:2] == "CV":
                        c = int(name[2])
                        act.wait_ge(conv, m * (DC * TAPS) + (c + 1) * TAPS)
                        nc.scalar.activation(dtu[:, p, c, :], xc[:, p, c, :], ACT.Tanh).then_inc(tanh_c, 1)
                    elif name[:2] == "XD":
                        q = int(name[2])
                        u = A_USES.index(name)
                        if q == 0 and not (isinstance(m, int) and m == 0):
                            act.wait_ge(b_out, m * 16)
                        full(act, aa_full, b, u)
                        nc.scalar.copy(xdT[:, q * 256:q * 256 + 256], aa[0:XD, u % 2, 0:256]).then_inc(aa_free[u % 2], 1)
                    elif name == "BOUT":
                        read_out(act, aa_free, b, A_USES.index("XD0"))
                        read_out(act, aa_free, b, A_USES.index("XD1"))
                        act.dma_start(bc_rows[bass.ds(m * (2 * NS), 2 * NS), :], xdT[RK:XD, :]).then_inc(b_out, 16)
                    elif name[:2] == "DT" and len(name) == 3 and name[2] != "U":
                        c = int(name[2])
                        u = A_USES.index(name)
                        if c == 0 and not (isinstance(m, int) and m < 2):
                            full(act, ac_full, before_c(m - 2), C_USES.index("M113"))
                        full(act, aa_full, b, u)
                        bias = par[:, P_DTB + c:P_DTB + c + 1]
                        nc.scalar.activation(dt[:, p, c, :], aa[:, u % 2, :], ACT.Abs, bias=bias).then_inc(softplus, 1)
                        nc.scalar.activation(dtu[:, p, c, :], aa[:, u % 2, :], ACT.Relu,
                                             bias=bias).then_inc(aa_free[u % 2], 1)
                    elif name == "SP":
                        act.wait_ge(softplus, m * (DC + 1) + DC)
                        nc.scalar.activation(dt[:, p, :, :], dt[:, p, :, :], ACT.Exp, scale=-1.0).then_inc(softplus, 1)
                        act.wait_ge(softplus, m * (DC + 1) + (DC + 1))
                        nc.scalar.activation(dt[:, p, :, :], dt[:, p, :, :], ACT.Ln, bias=1.0).then_inc(ln_done, 1)
                elif kind == "C":
                    b = before_c(m)
                    if name[0] == "Z":
                        u = C_USES.index(name)
                        full(act, ac_full, b, u)
                        nc.scalar.activation(th[:, u % 2, :], ac[:, u % 2, :], ACT.Tanh, scale=0.5).then_inc(z_tanh, 1)
                    elif name == "RMS":
                        act.wait_ge(rms, m * 6 + 6)
                        nc.scalar.activation(croot[:, :], croot[:, :], ACT.Sqrt).then_inc(c_root, 1)
                    elif name[:2] == "T1":
                        u = C_USES.index(name)
                        full(act, ac_full, b, u)
                        nc.scalar.copy(x1T(m, p)[:, int(name[2]), :], ac[:, u % 2, :]).then_inc(ac_free[u % 2], 1)
                    elif name[:2] == "M1":
                        u = C_USES.index(name)
                        full(act, ac_full, b, u)
                        nc.scalar.activation(th[:, u % 2, :], ac[:, u % 2, :], ACT.Tanh, scale=0.5).then_inc(m_tanh, 1)
                elif kind == "L" and name == "ROOT":
                    act.wait_ge(stats, 2 * NORM_STEPS + 2 * (NB - 2))
                    nc.scalar.activation(roots[:, :, NT:], roots[:, :, NT:], ACT.Sqrt).then_inc(ln_root, 1)
                elif kind == "R" and name[:2] == "TX":
                    g, k = int(name[2]), int(name[3])
                    u = g * KC + k
                    full(act, ac_full, 0, u)
                    nc.scalar.copy(xnT[g % 2][:, k, :], ac[:, u % 2, :]).then_inc(ac_free[u % 2], 1)
                elif kind == "R" and name == "RO0":
                    act.wait_ge(router, 3)
                    nc.scalar.activation(lg, lg, ACT.Exp).then_inc(router_exp, 1)
                elif kind == "D":
                    g = i
                    act.wait_ge(gathered[g % 2], 16 * 2 * NT * (g // 2 + 1))
                    for t in range(NT):
                        j = g * NT + t
                        last = nc.scalar.mul(gy[:, g % 2, 0, t, :], gy[:, g % 2, 0, t, :], gates[:, 0, j:j + 1])
                    last.then_inc(d_scaled, 1)
                    act.wait_ge(d_mixed, g + 1)
                    nc.scalar.activation(gy[:, g % 2, 0], gy[:, g % 2, 0], ACT.Silu).then_inc(d_gate, 1)
                elif kind == "M":
                    if name == "START":
                        for r in range(2):
                            full(act, mo_full, 0, 2 + r)
                            nc.scalar.copy(xsT[:, :, r:SLOTS:2], mo[:, r, 0:KC * P].rearrange("p (k t) -> p k t", k=KC)
                                           ).then_inc(mo_free[r], 1)
                        return
                    b = before_m(m)
                    if name[:2] == "UP":
                        pair = int(name[2])
                        u = i * len(M_USES) + M_USES.index(name)
                        full(act, mo_full, b, u)
                        for j in range(2):
                            hc = 2 * pair + j
                            last = nc.scalar.activation(hid[:, 0, hc, :], mo[:, u % 2, j * SLOTS:(j + 1) * SLOTS],
                                                        ACT.Relu, bias=w1[:, KC * HID + hc:KC * HID + hc + 1])
                        last.then_inc(mo_free[u % 2], 1)
                    elif name == "MT":
                        u = i * len(M_USES) + M_USES.index(name)
                        if is_last_tile(m, i):
                            return
                        full(act, mo_full, b, u)
                        nc.scalar.copy(xsT[:, :, :].rearrange("p k (t r) -> p k r t", r=2),
                                       mo[:, u % 2, :].rearrange("p (k r t) -> p k r t", k=KC, r=2)).then_inc(mo_free[u % 2], 1)
                    elif name[:2] == "DN":
                        r = int(name[2])
                        u = i * len(M_USES) + M_USES.index(name) - is_last_tile(m, i)
                        if r == 0:
                            act.wait_ge(ys_out[i % 2], (m - FIRST_BODY) * (16 * PER_BODY // 2) + (i // 2 * 16 + 16))
                        full(act, mo_full, b, u)
                        nc.scalar.copy(ys[:, i % 2, r, :], mo[:, u % 2, 0:DM]).then_inc(mo_free[u % 2], 1)
                        if r == 1:
                            tile = (m - FIRST_BODY) * PER_BODY + i
                            read_out(act, mo_free, b, u)
                            act.dma_start(slot_y_t[bass.ds(tile, 1)].rearrange("a p n -> p (a n)"),
                                          ys[:, i % 2, :, :].rearrange("p r d -> p (r d)")).then_inc(ys_out[i % 2], 16)

            walk(act, do, LATER["act"])

        @block.tensor
        def _(pe):
            pe.wait_ge(params_in, 64)
            pe.wait_ge(consts, CONSTS)
            def products(dst, lhs, rhs, n):
                for k in range(n):
                    last = pe.matmul(dst, lhs(k), rhs(k), start=(k == 0), stop=(k == n - 1))
                return last

            def transposes(dst, pieces):
                for j, src in enumerate(pieces):
                    last = pe.transpose(dst[:, j * P:j * P + P], src, ident[:, :])
                return last

            def do(kind, name, i, m, p):
                if kind == "A" and name in A_USES:
                    u = A_USES.index(name)
                    b = before_a(m)
                    dst = aa[:, u % 2, :]
                    if name[:2] == "TR":
                        k = int(name[2])
                        if k == 0:
                            pe.wait_ge(xr_ready, m + 1)
                        free(pe, aa_free, b, u)
                        last = transposes(dst, [xa[:, j, k * P:k * P + P] for j in range(NT)])
                    elif name[:2] == "IN":
                        c = int(name[2])
                        if c == 0:
                            read_out(pe, aa_free, b, A_USES.index("TR0"))
                            read_out(pe, aa_free, b, A_USES.index("TR1"))
                        free(pe, aa_free, b, u)
                        last = products(dst, lambda k: w_in[:, k, c * P:c * P + P], lambda k: xrT[:, p, k, :], KC)
                    elif name[:2] == "XD":
                        q = int(name[2])
                        if q == 0:
                            pe.wait_ge(xc_ready, m * DC + DC)
                        free(pe, aa_free, b, u)
                        last = products(dst[0:XD, 0:256], lambda c: par[:, P_XPROJ + c * XD:P_XPROJ + c * XD + XD],
                                        lambda c: xc[:, p, c, q * 256:q * 256 + 256], DC)
                    else:
                        c = int(name[2])
                        if c == 0:
                            read_out(pe, aa_free, b, A_USES.index("XD0"))
                            read_out(pe, aa_free, b, A_USES.index("XD1"))
                        free(pe, aa_free, b, u)
                        last = pe.matmul(dst, wdt[:, c * P:c * P + P], xdT[0:RK, :], start=True, stop=True)
                    last.then_inc(aa_full[u % 2], 1)
                elif kind == "R" and name[:2] == "TX":
                    g, k = int(name[2]), int(name[3])
                    u = g * KC + k
                    pe.wait_ge(xn_ready, g * NT + NT)
                    free(pe, ac_free, 0, u)
                    transposes(ac[:, u % 2, :], [xn_all[:, g * NT + j, k * P:k * P + P] for j in range(NT)]
                               ).then_inc(ac_full[u % 2], 1)
                elif kind == "R" and name[:2] == "LG":
                    g = int(name[2])
                    for k in range(KC):
                        read_out(pe, ac_free, 0, g * KC + k)
                    for t in range(g * NT, g * NT + NT):
                        j = t - g * NT
                        last = products(mo[:, 0, t * NE:t * NE + NE], lambda k: xnT[g % 2][:, k, j * P:j * P + P],
                                        lambda k: par[:, P_GATE + k * NE:P_GATE + k * NE + NE], KC)
                    if g == NB - 1:
                        last.then_inc(mo_full[0], 1)
                elif kind == "R" and name == "BL":
                    pe.wait_ge(router, 12)
                    pe.matmul(mo[:, 1, 0:AE], below[:, :], sel, start=True, stop=True)
                    pe.matmul(mo[:, 1, AE:2 * AE], ones[:, :], sel, start=True, stop=True).then_inc(mo_full[1], 1)
                elif kind == "C" and name in C_USES:
                    u = C_USES.index(name)
                    b = before_c(m)
                    dst = ac[:, u % 2, :]
                    if name[0] == "Z":
                        c = int(name[1]) + DC
                        free(pe, ac_free, b, u)
                        last = products(dst, lambda k: w_in[:, k, c * P:c * P + P], lambda k: xrT[:, p, k, :], KC)
                    elif name[:3] == "OUT":
                        if name == "OUT0":
                            read_out(pe, ac_free, b, C_USES.index("Z2"))
                            read_out(pe, ac_free, b, C_USES.index("Z3"))
                        free(pe, ac_free, b, u)
                        for r in range(2):
                            j = 2 * int(name[3]) + r
                            last = products(dst[:, r * DM:r * DM + DM], lambda c: xc[:, p, c, j * P:j * P + P],
                                            lambda c: w_out[:, c, :], DC)
                    elif name[:2] == "T1":
                        k = int(name[2])
                        if k == 0:
                            pe.wait_ge(x1r_ready, m + 1)
                        free(pe, ac_free, b, u)
                        last = transposes(dst, [xb[:, j, k * P:k * P + P] for j in range(NT)])
                    elif name[:2] == "M1":
                        q, pair = int(name[2]), int(name[3])
                        if q == 0 and pair == 0:
                            pe.wait_ge(wm_in, 16)
                            read_out(pe, ac_free, b, C_USES.index("T10"))
                            read_out(pe, ac_free, b, C_USES.index("T11"))
                        free(pe, ac_free, b, u)
                        for r in range(2):
                            hc = 2 * pair + r
                            last = products(dst[:, r * 256:r * 256 + 256], lambda k: wm1[:, k, hc * P:hc * P + P],
                                            lambda k: x1T(m, p)[:, k, q * 256:q * 256 + 256], KC)
                    else:
                        q, r = int(name[2]), int(name[3])
                        if r == 0:
                            read_out(pe, ac_free, b, C_USES.index("M1%d2" % q))
                            read_out(pe, ac_free, b, C_USES.index("M1%d3" % q))
                        free(pe, ac_free, b, u)
                        last = products(dst[:, 0:DM], lambda k: hid[:, 1, k, r * P:r * P + P], lambda k: wm2[:, k, :], HC)
                    last.then_inc(ac_full[u % 2], 1)
                elif kind == "M":
                    if name == "START":
                        pe.wait_ge(xs_in[0], 16)
                        for r in range(2):
                            free(pe, mo_free, 0, 2 + r)
                            transposes(mo[:, r, :], [xs[:, 0, r, k * P:k * P + P] for k in range(KC)]).then_inc(mo_full[r], 1)
                        return
                    if name == "NEXT":
                        return
                    b = before_m(m)
                    tile = (m - FIRST_BODY) * PER_BODY + i
                    last_tile = is_last_tile(m, i)
                    u = i * len(M_USES) + M_USES.index(name)
                    if name[:2] == "UP":
                        pair = int(name[2])
                        if pair == 0:
                            if i == 0:
                                read_out(pe, mo_free, b, -1)
                                read_out(pe, mo_free, b, -2)
                            else:
                                read_out(pe, mo_free, b, (i - 1) * len(M_USES) + M_USES.index("MT"))
                            pe.wait_ge(w1_in, tile * 16 + 16)
                        free(pe, mo_free, b, u)
                        for r in range(2):
                            hc = 2 * pair + r
                            last = products(mo[:, u % 2, r * SLOTS:(r + 1) * SLOTS], lambda k: w1v[:, k, hc * P:hc * P + P],
                                            lambda k: xsT[:, k, :], KC)
                    elif name == "MT":
                        if last_tile:
                            return
                        pe.wait_ge(xs_in[(i + 1) % 2],
                                   (m - FIRST_BODY) * (16 * PER_BODY // 2) + ((i + 1) // 2 * 16 + 16))
                        free(pe, mo_free, b, u)
                        last = transposes(mo[:, u % 2, :], [xs[:, (i + 1) % 2, r, k * P:k * P + P]
                                                            for k in range(KC) for r in range(2)])
                    else:
                        r = int(name[2])
                        if r == 0:
                            first_u = i * len(M_USES)
                            read_out(pe, mo_free, b, first_u + M_USES.index("UP2"))
                            read_out(pe, mo_free, b, first_u + M_USES.index("UP3"))
                            pe.wait_ge(w2_in, tile * 32 + 32)
                        u -= last_tile
                        free(pe, mo_free, b, u)
                        o = mo[:, u % 2, 0:DM]
                        for k in range(HC):
                            pe.matmul(o, hid[:, 0, k, r:SLOTS:2], w2[:, k, :], start=(k == 0), stop=False)
                        last = pe.matmul(o, ones[0:1, :], b2row[:, :], start=False, stop=True)
                    last.then_inc(mo_full[u % 2], 1)

            walk(pe, do)

        @block.vector
        def _(dve):
            for s_, v in ((aa_free[0], 1), (aa_free[1], 1), (ac_free[0], 1), (ac_free[1], 1), (mo_free[0], 1), (mo_free[1], 1), (scanned, DC),
                          (y_added, 2), (s_out, 16), (ys_out[0], 16), (ys_out[1], 16)):
                dve.sem_inc(s_, v)
            count = [0]

            def norm_step(ins):
                count[0] += 1
                ins.then_inc(stats, 1)
                dve.wait_ge(stats, count[0])

            def token_stats(g):
                dve.wait_ge(x_in[g], 16)
                for t in range(NT):
                    last = nc.vector.bn_stats(st[:, g * NT + t, :], xn_all[:, g * NT + t, :])
                norm_step(last)
                for t in range(NT):
                    last = nc.vector.bn_aggr(mv[:, g * NT + t, :], st[:, g * NT + t, :])
                norm_step(last)

            def norm_roots(a, b):
                norm_step(nc.vector.tensor_scalar(ms[:, a:b], mv[:, a:b, 1], LN_EPS, None, ALU.add))
                norm_step(nc.vector.reciprocal(roots[:, 0, a:b], ms[:, a:b]))
                norm_step(nc.vector.tensor_tensor(ms[:, a:b], mv[:, a:b, 1], roots[:, 0, a:b], ALU.mult))
                norm_step(nc.vector.tensor_scalar(ms[:, a:b], ms[:, a:b], RMS_EPS, None, ALU.add))
                norm_step(nc.vector.reciprocal(roots[:, 1, a:b], ms[:, a:b]))

            def norm(a, b):
                for t in range(a, b):
                    nc.vector.tensor_scalar(xn_all[:, t, :], xn_all[:, t, :], mv[:, t, 0:1], roots[:, 0, t:t + 1],
                                            ALU.subtract, ALU.mult).then_inc(xn_ready, 1)

            token_stats(0)
            norm_roots(0, NT)
            dve.wait_ge(ln_root, 1)
            norm(0, NT)
            dve.wait_ge(params_in, 64)
            dve.wait_ge(consts, CONSTS)
            nc.vector.tensor_scalar(par[:, P_CONVW:P_DTB], par[:, P_CONVW:P_DTB], 0.5, None, ALU.mult).then_inc(halved, 1)

            done = [0]

            def step(ins):
                done[0] += 1
                ins.then_inc(router, 1)
                dve.wait_ge(router, done[0])

            def by_te(a):
                return a.rearrange("p (t e) -> p t e", e=NE)

            def over_e(a, n=AT):
                return a.rearrange("p (t a) -> p t a", a=1).broadcast_to([P, n, NE])

            def over_t(a, n=AT):
                return a.rearrange("p (a e) -> p a e", a=1).broadcast_to([P, n, NE])

            c4 = cmp.rearrange("p (t e f) -> p t e f", e=NE, f=NE)
            t4 = tie.rearrange("p (t e f) -> p t e f", e=NE, f=NE)
            this = prob.rearrange("p (t e a) -> p t e a", e=NE, a=1).broadcast_to([P, AT, NE, NE])
            other = prob.rearrange("p (t a e) -> p t a e", e=NE, a=1).broadcast_to([P, AT, NE, NE])
            t3 = tie.rearrange("p (t f) -> p t f", f=NE * NE)
            eb = earlier.rearrange("p (a f) -> p a f", a=1).broadcast_to([P, AT, NE * NE])
            counts = incl.rearrange("p (e t) -> p e t", e=NE)[:, :, AT - 1:AT].broadcast_to([P, NE, 16])
            c3 = cnt.rearrange("p (e f) -> p e f", e=NE)
            i3 = incl.rearrange("p (e t) -> p e t", e=NE)

            def route(piece):
                if piece == 0:
                    full(dve, mo_full, 0, 0)
                    step(nc.vector.tensor_tensor(by_te(lg), by_te(mo[:, 0, 0:AE]), over_t(gateb), ALU.add))
                    step(nc.vector.tensor_reduce(red, by_te(lg), AX_X, ALU.max))
                    step(nc.vector.tensor_tensor(by_te(lg), by_te(lg), over_e(red), ALU.subtract))
                    dve.sem_inc(mo_free[0], 1)
                elif piece == 1:
                    dve.wait_ge(router_exp, 1)
                    step(nc.vector.tensor_reduce(red, by_te(lg), AX_X, ALU.add))
                    step(nc.vector.reciprocal(red, red))
                    step(nc.vector.tensor_tensor(by_te(prob), by_te(lg), over_e(red), ALU.mult))
                elif piece == 2:
                    nc.vector.tensor_tensor(c4, other, this, ALU.is_gt)
                    step(nc.vector.tensor_tensor(t4, other, this, ALU.is_equal))
                    step(nc.vector.tensor_tensor(t3, t3, eb, ALU.mult))
                elif piece == 3:
                    step(nc.vector.tensor_tensor(cmp, cmp, tie, ALU.add))
                    step(nc.vector.tensor_reduce(rank, cmp.rearrange("p (t f) -> p t f", f=NE), AX_X, ALU.add))
                    nc.vector.tensor_scalar(m0, rank, 0.0, None, ALU.is_equal)
                    nc.vector.tensor_scalar(m1, rank, 1.0, None, ALU.is_equal)
                    step(nc.vector.tensor_scalar(sel, rank, 1.5, None, ALU.is_lt))
                    step(nc.vector.tensor_tensor(rank, m0, prob, ALU.mult))
                    step(nc.vector.tensor_reduce(gates[:, 0, :], by_te(rank), AX_X, ALU.add))
                    step(nc.vector.tensor_tensor(rank, m1, prob, ALU.mult))
                    step(nc.vector.tensor_reduce(gates[:, 1, :], by_te(rank), AX_X, ALU.add))
                elif piece == 4:
                    full(dve, mo_full, 0, 1)
                    step(nc.vector.tensor_copy(tot.rearrange("p (e t) -> p e t", e=NE),
                                               mo[:, 1, AE:2 * AE].rearrange("p (t e) -> p e t", e=NE)))
                    step(nc.vector.tensor_tensor_scan(incl, seg, tot, 0.0, ALU.mult, ALU.add))
                    step(nc.vector.tensor_tensor(c3, counts, steps.rearrange("p (a f) -> p a f", a=1).broadcast_to([P, NE, 16]),
                                                 ALU.is_gt))
                elif piece == 5:
                    step(nc.vector.tensor_reduce(ntile, c3, AX_X, ALU.add))
                    step(nc.vector.tensor_tensor_scan(ends, ones[:, 0:NE], ntile, 0.0, ALU.mult, ALU.add))
                    step(nc.vector.tensor_tensor(base_, ends, ntile, ALU.subtract))
                    step(nc.vector.tensor_tensor(incl, incl, tot, ALU.subtract))
                    step(nc.vector.scalar_tensor_tensor(
                        out=i3, in0=base_.rearrange("p (e a) -> p e a", a=1).broadcast_to([P, NE, AT]), scalar=float(SLOTS),
                        in1=i3, op0=ALU.mult, op1=ALU.add))
                elif piece == 6:
                    step(nc.vector.tensor_tensor(by_te(slotf), by_te(mo[:, 1, 0:AE]), incl.rearrange("p (e t) -> p t e", e=NE),
                                                 ALU.add))
                    dve.sem_inc(mo_free[1], 1)
                    step(nc.vector.tensor_tensor(m0, m0, slotf, ALU.mult))
                    step(nc.vector.tensor_tensor(m1, m1, slotf, ALU.mult))
                    step(nc.vector.tensor_reduce(red, by_te(m0), AX_X, ALU.add))
                    step(nc.vector.tensor_copy(slots[:, 0, :], red))
                    step(nc.vector.tensor_reduce(red, by_te(m1), AX_X, ALU.add))
                    step(nc.vector.tensor_copy(slots[:, 1, :], red))
                elif piece == 7:
                    step(nc.vector.tensor_tensor(ecmp.rearrange("p (t e) -> p t e", e=NE), over_e(ti, ZTILES),
                                                 over_t(ends, ZTILES), ALU.is_ge))
                    step(nc.vector.tensor_reduce(ef, ecmp.rearrange("p (t e) -> p t e", e=NE), AX_X, ALU.add))
                    step(nc.vector.tensor_scalar(ef, ef, float(NE - 1), None, ALU.min))
                    nc.vector.tensor_copy(eid[:, :], ef).then_inc(routed, 1)
                    dve.wait_ge(routed, 1)
                    dve.sem_inc(routed, 1)

            def do(kind, name, i, m, p):
                if kind == "L":
                    if name == "ROOT":
                        norm_roots(NT, AT)
                    elif name == "XN":
                        dve.wait_ge(ln_root, 2)
                        norm(NT, AT)
                    else:
                        token_stats(int(name[1]))
                elif kind == "R" and name[:2] == "RO":
                    route(int(name[2]))
                elif kind == "S" and name == "SCAN":
                    s, c = i
                    if s == 0 and c == 0 and not (isinstance(m, int) and m == 0):
                        dve.wait_ge(carried, m * NS)
                        apart(dve)
                    if s >= 2 or not (isinstance(m, int) and m == 0):
                        wait_hc(dve, m, s - 2, (c,))
                        apart(dve)
                    dve.wait_ge(decay_ready, m * (NS * DC) + (s * DC + c + 1))
                    wait_dbu(dve, m, s, (c,))
                    nc.vector.tensor_tensor_scan(h[:, s % 2, c, :], decay[:, c % 2, :], dbu[:, c, :],
                                                 carry[:, p, s * DC + c:s * DC + c + 1], ALU.mult, ALU.add
                                                 ).then_inc(scanned, 1)
                    if c + 1 in OWN_DBU:
                        if s == 0 and c + 1 == OWN_DBU[0]:
                            dve.wait_ge(dtu_ready, m + 1)
                            apart(dve)
                        if c + 1 == OWN_DBU[0]:
                            dve.wait_ge(bb_in[s % 2], m * (NS * 8) + (s // 2 * 16 + 16))
                            apart(dve)
                        dve.wait_ge(scanned, m * (NS * DC) + (s * DC + c + 2))
                        nc.vector.tensor_tensor(dbu[:, c + 1, :], dtu[:, p, c + 1, :], bb[:, s % 2, :],
                                                ALU.mult).then_inc(own_dbu_ready, 1)
                elif kind == "S":
                    s = i[0]
                    dve.wait_ge(scanned, m * (NS * DC) + (s * DC + DC + DC))
                    nc.vector.tensor_copy(carry[:, p, s * DC:s * DC + DC], h[:, s % 2, :, BT - 1]).then_inc(carried, 1)
                elif kind == "Y":
                    s, c = i
                    wait_hc(dve, m, s, (c,))
                    if s == 0:
                        nc.vector.scalar_tensor_tensor(out=xc[:, p, c, :], in0=xc[:, p, c, :],
                                                       scalar=par[:, P_D + c:P_D + c + 1], in1=hxc[:, c % 2, :],
                                                       op0=ALU.mult, op1=ALU.add).then_inc(y_added, 1)
                    else:
                        nc.vector.tensor_tensor(xc[:, p, c, :], xc[:, p, c, :], hxc[:, c % 2, :],
                                                ALU.add).then_inc(y_added, 1)
                    if c + 1 in OWN_HC:
                        if c + 1 == OWN_HC[0]:
                            dve.wait_ge(cb_in[s % 2], m * (NS * 8) + (s // 2 * 16 + 16))
                            apart(dve)
                        dve.wait_ge(scanned, m * (NS * DC) + (s * DC + c + 2 + DC))
                        apart(dve)
                        dve.wait_ge(y_added, m * (NS * DC) + (s * DC + c + 2))
                        nc.vector.tensor_tensor(hxc[:, (c + 1) % 2, :], h[:, s % 2, c + 1, :], cb[:, s % 2, :],
                                                ALU.mult).then_inc(own_hc_ready, 1)
                elif kind == "A":
                    b = before_a(m)
                    if name == "XR":
                        first = isinstance(m, int) and m == 0
                        if first:
                            dve.wait_ge(xn_ready, NT)
                        else:
                            dve.wait_ge(xa_in, m * 16)
                        for t in range(NT):
                            rows = xn_all[:, t, :] if first else xa[:, t, :]
                            last = nc.vector.tensor_scalar(xa[:, t, :], rows, roots[:, 1, bass.ds(m * NT + t, 1)],
                                                           None, ALU.mult)
                        last.then_inc(xr_ready, 1)
                    elif name == "HALO":
                        if not isinstance(m, int) or m >= 2:
                            dve.wait_ge(halo_kept, m)
                        nc.vector.tensor_copy(xpad[:, :, 0:TAPS - 1], halo[:, p, :, :]).then_inc(halo_in, 1)
                    elif name[:2] == "CV":
                        c = int(name[2])
                        read_out(dve, aa_free, b, A_USES.index("IN%d" % c))
                        if c == 0:
                            dve.wait_ge(halo_in, m + 1)
                            dve.wait_ge(halved, 1)
                            if not (isinstance(m, int) and m < 2):
                                full(dve, ac_full, before_c(m - 2), C_USES.index("OUT1"))
                        w = [par[:, P_CONVW + c * TAPS + k:P_CONVW + c * TAPS + k + 1] for k in range(TAPS)]
                        nc.vector.tensor_scalar(xc[:, p, c, :], xpad[:, c, 0:BT], w[0], par[:, P_CONVB + c:P_CONVB + c + 1],
                                                ALU.mult, ALU.add).then_inc(conv, 1)
                        for k in range(1, TAPS):
                            dve.wait_ge(conv, m * (DC * TAPS) + (c * TAPS + k))
                            nc.vector.scalar_tensor_tensor(out=xc[:, p, c, :], in0=xpad[:, c, k:k + BT], scalar=w[k],
                                                           in1=xc[:, p, c, :], op0=ALU.mult, op1=ALU.add).then_inc(conv, 1)
                    elif name[:2] == "SL":
                        c = int(name[2])
                        dve.wait_ge(tanh_c, m * DC + (c + 1))
                        nc.vector.scalar_tensor_tensor(out=xc[:, p, c, :], in0=dtu[:, p, c, :], scalar=1.0,
                                                       in1=xc[:, p, c, :], op0=ALU.add, op1=ALU.mult).then_inc(xc_ready, 1)
                    elif name == "HKEEP":
                        nc.vector.tensor_copy(halo[:, p, :, :], xpad[:, :, BT:BT + TAPS - 1]).then_inc(halo_kept, 1)
                    elif name == "DT":
                        dve.wait_ge(ln_done, m + 1)
                        nc.vector.tensor_tensor(dt[:, p, :, :], dt[:, p, :, :], dtu[:, p, :, :], ALU.add).then_inc(dt_ready, 1)
                    elif name == "DTU":
                        dve.wait_ge(dt_ready, m + 1)
                        nc.vector.tensor_tensor(dtu[:, p, :, :], dt[:, p, :, :], xc[:, p, :, :], ALU.mult).then_inc(dtu_ready, 1)
                elif kind == "C":
                    b = before_c(m)
                    if name[0] == "Z":
                        c = int(name[1])
                        u = C_USES.index(name)
                        dve.wait_ge(z_tanh, m * DC + (c + 1))
                        nc.vector.scalar_tensor_tensor(out=th[:, u % 2, :], in0=th[:, u % 2, :], scalar=1.0,
                                                       in1=ac[:, u % 2, :], op0=ALU.add, op1=ALU.mult).then_inc(z_silu, 1)
                        dve.wait_ge(z_silu, m * DC + (c + 1))
                        dve.wait_ge(y_added, m * (NS * DC) + ((NS - 1) * DC + c + 1 + 2))
                        nc.vector.scalar_tensor_tensor(out=xc[:, p, c, :], in0=th[:, u % 2, :], scalar=0.5,
                                                       in1=xc[:, p, c, :], op0=ALU.mult, op1=ALU.mult
                                                       ).then_inc(ac_free[u % 2], 1)
                    elif name[:3] == "OUT":
                        u = C_USES.index(name)
                        t = 2 * int(name[3])
                        if t == 0:
                            dve.wait_ge(x1_in, m * 16 + 16)
                        full(dve, ac_full, b, u)
                        nc.vector.tensor_tensor(x1[:, t:t + 2, :], x1[:, t:t + 2, :],
                                                ac[:, u % 2, :].rearrange("p (t d) -> p t d", t=2), ALU.add
                                                ).then_inc(ac_free[u % 2], 1)
                    elif name == "RMS":
                        read_out(dve, ac_free, b, C_USES.index("OUT0"))
                        read_out(dve, ac_free, b, C_USES.index("OUT1"))
                        for t in range(NT):
                            last = nc.vector.bn_stats(cst[:, t, :], x1[:, t, :])
                        last.then_inc(rms, 1)
                        dve.wait_ge(rms, m * 6 + 1)
                        apart(dve)
                        for t in range(NT):
                            last = nc.vector.bn_aggr(cmv[:, t, :], cst[:, t, :])
                        last.then_inc(rms, 1)
                        dve.wait_ge(rms, m * 6 + 2)
                        nc.vector.tensor_tensor(cms[:, :], cmv[:, :, 0], cmv[:, :, 0], ALU.mult).then_inc(rms, 1)
                        dve.wait_ge(rms, m * 6 + 3)
                        nc.vector.tensor_tensor(cms[:, :], cms[:, :], cmv[:, :, 1], ALU.add).then_inc(rms, 1)
                        dve.wait_ge(rms, m * 6 + 4)
                        nc.vector.tensor_scalar(cms[:, :], cms[:, :], RMS_EPS, None, ALU.add).then_inc(rms, 1)
                        dve.wait_ge(rms, m * 6 + 5)
                        nc.vector.reciprocal(croot[:, :], cms[:, :]).then_inc(rms, 1)
                    elif name == "NORM":
                        dve.wait_ge(c_root, m + 1)
                        for t in range(NT):
                            last = nc.vector.tensor_scalar(xb[:, t, :], x1[:, t, :], croot[:, t:t + 1], None, ALU.mult)
                        last.then_inc(x1r_ready, 1)
                    elif name[:2] == "M1":
                        q, pair = int(name[2]), int(name[3])
                        u = C_USES.index(name)
                        if q == 0 and pair == 0:
                            dve.wait_ge(scattered, 16 * 2 * AT)
                        dve.wait_ge(m_tanh, m * HC + (q * (HC // 2) + pair + 1))
                        nc.vector.scalar_tensor_tensor(
                            out=hid[:, 1, 2 * pair:2 * pair + 2, :].rearrange("p r t -> p (r t)"), in0=th[:, u % 2, :],
                            scalar=1.0, in1=ac[:, u % 2, :], op0=ALU.add, op1=ALU.mult).then_inc(ac_free[u % 2], 1)
                    elif name[:2] == "M2":
                        q, r = int(name[2]), int(name[3])
                        u = C_USES.index(name)
                        full(dve, ac_full, b, u)
                        nc.vector.scalar_tensor_tensor(out=x1[:, 2 * q + r, :], in0=ac[:, u % 2, 0:DM], scalar=0.5,
                                                       in1=x1[:, 2 * q + r, :], op0=ALU.mult, op1=ALU.add
                                                       ).then_inc(ac_free[u % 2], 1)

                elif kind == "D":
                    g = i
                    b = g % 2
                    dve.wait_ge(d_scaled, g + 1)
                    for t in range(NT):
                        j = g * NT + t
                        last = nc.vector.scalar_tensor_tensor(out=gy[:, b, 0, t, :], in0=gy[:, b, 1, t, :],
                                                              scalar=gates[:, 1, j:j + 1], in1=gy[:, b, 0, t, :],
                                                              op0=ALU.mult, op1=ALU.add)
                    last.then_inc(d_mixed, 1)
                    if g >= 1:
                        finish(dve, g - 1)

            walk(dve, do, LATER["dve"])
            finish(dve, NB - 1)


def kernel(**inputs):
    import numpy as np
    import concourse.bacc as bacc
    from concourse.bass_utils import run_bass_kernel_spmd

    def a(name):
        return np.asarray(inputs[name])

    def rows(m):
        k = m.shape[0] // P
        return m.reshape(k, P, -1).transpose(1, 0, 2).reshape(P, -1)

    arrays = {
        "x": a("L0_attn_x").reshape(BATCH * SEQ, DM),
        "params": np.concatenate([
            rows(a("L0_attn_conv_w")), rows(a("L0_attn_conv_b").reshape(DI, 1)), rows(a("L0_attn_dt_proj_b").reshape(DI, 1)),
            rows(a("L0_attn_D").reshape(DI, 1)), a("L0_attn_A_log").reshape(DC, P, NS).transpose(1, 2, 0).reshape(P, -1),
            rows(a("L0_ffn_gate_w")), rows(a("L0_attn_x_proj_w").T)], axis=1),
        "weights": np.concatenate([rows(a("L0_attn_in_proj_w").T), rows(a("L0_attn_out_proj_w").T)], axis=1),
        "w_dt": a("L0_attn_dt_proj_w").T,
        "moe1": np.stack([np.concatenate([rows(a("L0_ffn_w1")[e]), rows(a("L0_ffn_b1")[e].reshape(HID, 1))], axis=1)
                          for e in range(NE)]),
        "moe2": np.stack([rows(a("L0_ffn_w2")[e]) for e in range(NE)]),
        "moe_b2": a("L0_ffn_b2"),
        "gate_b": a("L0_ffn_gate_b"),
        "mlp": np.concatenate([rows(a("L0_attn_mlp_w1").T), rows(a("L0_attn_mlp_w2").T)], axis=1),
    }
    arrays = {k: np.ascontiguousarray(v) for k, v in arrays.items()}
    nc = bacc.Bacc("TRN2", target_bir_lowering=False, num_devices=1)
    args = [nc.dram_tensor(k, v.shape, F32, kind="ExternalInput").ap() for k, v in arrays.items()]
    out = nc.dram_tensor("out", (BATCH * SEQ, DM), F32, kind="ExternalOutput").ap()

    def scratch(name, shape):
        return nc.dram_tensor(name, shape, F32, kind="Internal").ap()

    mamba_moe(nc, *args, out, scratch("bc_rows", (NB * 2 * NS, BT)), scratch("xn_rows", (BATCH * SEQ, DM)),
              scratch("s_rows", (BATCH * SEQ, DM)), scratch("slot_x", (ZTILES * SLOTS, DM)),
              scratch("slot_y", (TILES * SLOTS, DM)))
    r = run_bass_kernel_spmd(nc, [arrays], core_ids=[0])
    return r.results[0]["out"].reshape(BATCH, SEQ, DM)
```
